# Optimizing a Trainium2 kernel written in Bass

```python
import numpy as np
import jax
import jax.numpy as jnp

def _softmax(x, axis=-1):
    return jax.nn.softmax(x, axis=axis)

def _gelu(x):
    return jax.nn.gelu(x, approximate=True)

def _silu(x):
    return jax.nn.silu(x)

def _sigmoid(x):
    return jax.nn.sigmoid(x)

def _layernorm(x, axis=-1, eps=1e-05):
    m = jnp.mean(x, axis=axis, keepdims=True)
    v = jnp.var(x, axis=axis, keepdims=True)
    return (x - m) / jnp.sqrt(v + eps)

def _scatter_add(tgt, idx, src, axis=0):
    return tgt.at[idx].add(src)

def _segment_sum(src, seg, n):
    return jax.ops.segment_sum(src, seg, n)
kernel_name = 'mk_prb_d1_jaxref_r4_cb0548'

def setup_inputs(seed: int=0):
    np.random.seed(seed)
    _w = jnp.asarray

    def _L0_attn_setup():
        import jax, jax.numpy as jnp
        import numpy as np
        D_MODEL = 256
        D_STATE = 128
        D_CONV = 4
        EXPAND = 2
        HEADDIM = 64
        D_INNER = EXPAND * D_MODEL
        NHEADS = D_INNER // HEADDIM
        NGROUPS = 1
        CONV_DIM = D_INNER + 2 * NGROUPS * D_STATE
        D_IN_PROJ = 2 * D_INNER + 2 * NGROUPS * D_STATE + NHEADS
        CHUNK = 64
        BATCH, SEQLEN = (4, 512)
        EPS = 1e-05

        def _segsum_exp(x):
            T = x.shape[-1]
            cs = jnp.cumsum(x, axis=-1)
            seg = cs[..., :, None] - cs[..., None, :]
            mask = jnp.tril(jnp.ones((T, T), dtype=bool))
            return jnp.where(mask, jnp.exp(jnp.where(mask, seg, 0.0)), 0.0)

        def _causal_conv(x, w, b):
            xt = jnp.transpose(x, (0, 2, 1))
            out = jax.lax.conv_general_dilated(xt, w[:, None, :], (1,), [(w.shape[-1] - 1, 0)], dimension_numbers=('NCH', 'OIH', 'NCH'), feature_group_count=w.shape[0])
            return jnp.transpose(out, (0, 2, 1)) + b

        def _ssd(X, A, B, C):
            b, l, h, p = X.shape
            c, Q = (l // CHUNK, CHUNK)
            X = X.reshape(b, c, Q, h, p)
            A = jnp.transpose(A.reshape(b, c, Q, h), (0, 3, 1, 2))
            B = B.reshape(b, c, Q, -1)
            C = C.reshape(b, c, Q, -1)
            A_cum = jnp.cumsum(A, axis=-1)
            L = _segsum_exp(A)
            Y_diag = jnp.einsum('bcln,bcsn,bhcls,bcshp->bclhp', C, B, L, X)
            decay_states = jnp.exp(A_cum[..., -1:] - A_cum)
            states = jnp.einsum('bcln,bhcl,bclhp->bchpn', B, decay_states, X)
            A_sum = jnp.pad(A_cum[..., -1], ((0, 0), (0, 0), (1, 0)))
            decay_chunk = _segsum_exp(A_sum)
            states = jnp.concatenate([jnp.zeros_like(states[:, :1]), states], axis=1)
            prev = jnp.einsum('bhzc,bchpn->bzhpn', decay_chunk, states)[:, :-1]
            Y_off = jnp.einsum('bcln,bchpn,bhcl->bclhp', C, prev, jnp.exp(A_cum))
            return (Y_diag + Y_off).reshape(b, l, h, p)
        key = jax.random.key(seed)
        ks = jax.random.split(key, 8)
        return {'hidden_states': jax.random.normal(ks[0], (BATCH, SEQLEN, D_MODEL), jnp.float32), 'W_in': jax.random.normal(ks[1], (D_MODEL, D_IN_PROJ), jnp.float32) * D_MODEL ** (-0.5), 'conv_w': jax.random.normal(ks[2], (CONV_DIM, D_CONV), jnp.float32) * 0.2, 'conv_b': jnp.zeros((CONV_DIM,), jnp.float32), 'dt_bias': jax.random.normal(ks[3], (NHEADS,), jnp.float32) * 0.1, 'A_log': jnp.log(jnp.arange(1, NHEADS + 1, dtype=jnp.float32)), 'D': jnp.ones((NHEADS,), jnp.float32), 'rms_w': jnp.ones((D_INNER,), jnp.float32), 'W_out': jax.random.normal(ks[4], (D_INNER, D_MODEL), jnp.float32) * D_INNER ** (-0.5), 'ln_g': jnp.ones((D_MODEL,), jnp.float32), 'ln_b': jnp.zeros((D_MODEL,), jnp.float32)}
    _L0_attn_in = _L0_attn_setup()

    def _L0_ffn_setup():
        import jax, jax.numpy as jnp
        import numpy as np
        D_MODEL = 256
        key = jax.random.key(seed)
        k_x, k_w, k_a1, k_a2 = jax.random.split(key, 4)
        x = jax.random.normal(k_x, (4, 512, D_MODEL), dtype=jnp.float32)
        weight = jax.random.normal(k_w, (D_MODEL, D_MODEL), dtype=jnp.float32) * 0.02
        aux_weight1 = jax.random.normal(k_a1, (D_MODEL, D_MODEL), dtype=jnp.float32) * 0.02
        aux_weight2 = jax.random.normal(k_a2, (D_MODEL, D_MODEL), dtype=jnp.float32) * 0.02
        bias = jnp.zeros((D_MODEL,), dtype=jnp.float32)
        return {'x': x, 'weight': weight, 'aux_weight1': aux_weight1, 'aux_weight2': aux_weight2, 'bias': bias}
    _L0_ffn_in = _L0_ffn_setup()
    _d = {'L0_attn_hidden_states': _L0_attn_in['hidden_states'], 'L0_attn_W_in': _L0_attn_in['W_in'], 'L0_attn_conv_w': _L0_attn_in['conv_w'], 'L0_attn_conv_b': _L0_attn_in['conv_b'], 'L0_attn_dt_bias': _L0_attn_in['dt_bias'], 'L0_attn_A_log': _L0_attn_in['A_log'], 'L0_attn_D': _L0_attn_in['D'], 'L0_attn_rms_w': _L0_attn_in['rms_w'], 'L0_attn_W_out': _L0_attn_in['W_out'], 'L0_attn_ln_g': _L0_attn_in['ln_g'], 'L0_attn_ln_b': _L0_attn_in['ln_b'], 'L0_ffn_weight': _L0_ffn_in['weight'], 'L0_ffn_aux_weight1': _L0_ffn_in['aux_weight1'], 'L0_ffn_aux_weight2': _L0_ffn_in['aux_weight2'], 'L0_ffn_bias': _L0_ffn_in['bias']}
    _x0 = _d['L0_attn_hidden_states']
    _d['L0_attn_hidden_states'] = jax.random.normal(jax.random.fold_in(jax.random.key(seed), 1), (2, 4096, 256), dtype=_x0.dtype)
    del _x0
    return _d

def reference(L0_attn_hidden_states, L0_attn_W_in, L0_attn_conv_w, L0_attn_conv_b, L0_attn_dt_bias, L0_attn_A_log, L0_attn_D, L0_attn_rms_w, L0_attn_W_out, L0_attn_ln_g, L0_attn_ln_b, L0_ffn_weight, L0_ffn_aux_weight1, L0_ffn_aux_weight2, L0_ffn_bias):

    def _L0_attn_ref(hidden_states, W_in, conv_w, conv_b, dt_bias, A_log, D, rms_w, W_out, ln_g, ln_b):
        import jax, jax.numpy as jnp
        import numpy as np
        D_MODEL = 256
        D_STATE = 128
        D_CONV = 4
        EXPAND = 2
        HEADDIM = 64
        D_INNER = EXPAND * D_MODEL
        NHEADS = D_INNER // HEADDIM
        NGROUPS = 1
        CONV_DIM = D_INNER + 2 * NGROUPS * D_STATE
        D_IN_PROJ = 2 * D_INNER + 2 * NGROUPS * D_STATE + NHEADS
        CHUNK = 64
        BATCH, SEQLEN = (4, 512)
        EPS = 1e-05

        def _segsum_exp(x):
            T = x.shape[-1]
            cs = jnp.cumsum(x, axis=-1)
            seg = cs[..., :, None] - cs[..., None, :]
            mask = jnp.tril(jnp.ones((T, T), dtype=bool))
            return jnp.where(mask, jnp.exp(jnp.where(mask, seg, 0.0)), 0.0)

        def _causal_conv(x, w, b):
            xt = jnp.transpose(x, (0, 2, 1))
            out = jax.lax.conv_general_dilated(xt, w[:, None, :], (1,), [(w.shape[-1] - 1, 0)], dimension_numbers=('NCH', 'OIH', 'NCH'), feature_group_count=w.shape[0])
            return jnp.transpose(out, (0, 2, 1)) + b

        def _ssd(X, A, B, C):
            b, l, h, p = X.shape
            c, Q = (l // CHUNK, CHUNK)
            X = X.reshape(b, c, Q, h, p)
            A = jnp.transpose(A.reshape(b, c, Q, h), (0, 3, 1, 2))
            B = B.reshape(b, c, Q, -1)
            C = C.reshape(b, c, Q, -1)
            A_cum = jnp.cumsum(A, axis=-1)
            L = _segsum_exp(A)
            Y_diag = jnp.einsum('bcln,bcsn,bhcls,bcshp->bclhp', C, B, L, X)
            decay_states = jnp.exp(A_cum[..., -1:] - A_cum)
            states = jnp.einsum('bcln,bhcl,bclhp->bchpn', B, decay_states, X)
            A_sum = jnp.pad(A_cum[..., -1], ((0, 0), (0, 0), (1, 0)))
            decay_chunk = _segsum_exp(A_sum)
            states = jnp.concatenate([jnp.zeros_like(states[:, :1]), states], axis=1)
            prev = jnp.einsum('bhzc,bchpn->bzhpn', decay_chunk, states)[:, :-1]
            Y_off = jnp.einsum('bcln,bchpn,bhcl->bclhp', C, prev, jnp.exp(A_cum))
            return (Y_diag + Y_off).reshape(b, l, h, p)
        residual = hidden_states
        zxbcdt = hidden_states @ W_in
        z, xBC, dt = jnp.split(zxbcdt, [D_INNER, D_INNER + CONV_DIM], axis=-1)
        dt = jax.nn.softplus(dt + dt_bias)
        xBC = jax.nn.silu(_causal_conv(xBC, conv_w, conv_b))
        x, B, C = jnp.split(xBC, [D_INNER, D_INNER + NGROUPS * D_STATE], axis=-1)
        b, l, _ = x.shape
        x = x.reshape(b, l, NHEADS, HEADDIM)
        a = -jnp.exp(A_log)
        y = _ssd(x * dt[..., None], dt * a, B, C)
        y = y + x * D[None, None, :, None]
        y = y.reshape(b, l, D_INNER)
        y = y * jax.nn.silu(z)
        y = y * jax.lax.rsqrt(jnp.mean(y * y, axis=-1, keepdims=True) + EPS) * rms_w
        out = y @ W_out
        h = residual + out
        mu = jnp.mean(h, axis=-1, keepdims=True)
        var = jnp.mean((h - mu) ** 2, axis=-1, keepdims=True)
        return (h - mu) * jax.lax.rsqrt(var + EPS) * ln_g + ln_b

    def _L0_ffn_ref(x, weight, aux_weight1, aux_weight2, bias):
        import jax, jax.numpy as jnp
        import numpy as np
        D_MODEL = 256
        h = jnp.einsum('btc,cd->btd', x, weight)
        h = jnp.einsum('btc,cd->btd', h, aux_weight1)
        h = jnp.einsum('btc,cd->btd', h, aux_weight2)
        return jnp.tanh(h + bias)
    x = L0_attn_hidden_states
    xn = _layernorm(x, axis=-1)
    x = x + _L0_attn_ref(xn, L0_attn_W_in, L0_attn_conv_w, L0_attn_conv_b, L0_attn_dt_bias, L0_attn_A_log, L0_attn_D, L0_attn_rms_w, L0_attn_W_out, L0_attn_ln_g, L0_attn_ln_b) + _L0_ffn_ref(xn, L0_ffn_weight, L0_ffn_aux_weight1, L0_ffn_aux_weight2, L0_ffn_bias)
    return x

_drawn_inputs = setup_inputs


def setup_inputs(seed=0):
    import zlib

    import numpy as np

    out = dict(_drawn_inputs(seed))
    spreads = {'L0_attn_conv_b': (0.0, 0.1),
     'L0_attn_D': (1.0, 0.2),
     'L0_attn_rms_w': (1.0, 0.2),
     'L0_attn_ln_g': (1.0, 0.2),
     'L0_attn_ln_b': (0.0, 0.1),
     'L0_ffn_bias': (0.0, 0.1)}
    factors = {'L0_attn_dt_bias': 4.486,
     'L0_ffn_weight': 3.306,
     'L0_ffn_aux_weight1': 3.313,
     'L0_ffn_aux_weight2': 3.303}
    for name, (base, spread) in spreads.items():
        noise = np.random.default_rng([zlib.crc32(name.encode()), seed]).standard_normal(out[name].shape)
        drawn = base * np.exp(spread * noise) if base else spread * noise
        out[name] = jnp.asarray(drawn.astype(out[name].dtype))
    for name, factor in factors.items():
        out[name] = (out[name] * factor).astype(out[name].dtype)
    return out
```

```python
from contextlib import ExitStack

import numpy as np

import concourse.bass as bass
from concourse import mybir

F32 = mybir.dt.float32
F32R = mybir.dt.float32r
ALU = mybir.AluOpType
ACT = mybir.ActivationFunctionType

P = 128
D = 256
DI = 512
H = 8
HD = DI // H
NS = 128
CONV = DI + 2 * NS
TAPS = 4
KD = D // P
KI = DI // P
CT = CONV // P
NG = CT // 2
Q = 2
HALO = TAPS - 1
EPS = 1e-5
BIG = -1e30
BUF = 3
FB = D + H
ZC, CC, FC = 0, DI, DI + CONV
WC = FC + FB
LO = 32
LOG_TERMS = 7


def log1p_coefficients():
    w = (1 - np.cos(np.pi * (np.arange(64) + 0.5) / 64)) / 18
    s = np.sqrt(w)
    fit = np.polynomial.Chebyshev.fit(w, 2 * np.arctanh(s) / s, LOG_TERMS - 1, domain=[0, 1 / 9])
    return [float(c) for c in fit.convert(kind=np.polynomial.Polynomial).coef]


def program(nc, x, w_in, conv_w, conv_b, dt_bias, a_log, d_skip, rms_w, w_out, ln_g, ln_b,
            f1t, f2t, f3, f_bias, out):
    steps = x.shape[1] // P
    x_t = x.rearrange("q t d -> t q d")
    out_t = out.rearrange("q t d -> t q d")
    logc = log1p_coefficients()

    with ExitStack() as ctx:
        def sb(name, shape, dt=F32):
            return ctx.enter_context(nc.sbuf_tensor(name, shape, dt))

        def sem(name):
            return ctx.enter_context(nc.semaphore(name))

        def sems(name, n):
            return [sem(f"{name}{i}") for i in range(n)]

        ring0, ring1, e_bank0, e_bank1, xt_bank, bg_bank, yoff_bank, yd_bank = [
            ctx.enter_context(nc.psum_tensor(n, [P, 512], F32))
            for n in ("ring0", "ring1", "e_bank0", "e_bank1", "xt_bank", "bg_bank", "yoff_bank", "yd_bank")]
        e_bank = [e_bank0, e_bank1]

        nw = KD * (DI + CONV + H)
        lay1 = sb("lay1", [P, 2 * Q * H * P])
        lay2 = sb("lay2", [P, 4 * Q * DI])
        win = lay1[:, 0:nw].rearrange("p (k n) -> p k n", k=KD)
        wh = sb("wh", [P, KD, WC], F32R)
        wl = sb("wl", [P, KD, WC], F32R)
        nf = KD * D
        nsel = 2 * H * P
        f1s = lay1[:, nw:nw + nf].rearrange("p (k n) -> p k n", k=KD)
        f2s = lay1[:, nw + nf:nw + 2 * nf].rearrange("p (k n) -> p k n", k=KD)
        sel = lay2[0:LO + 2 * H, 0:nsel].rearrange("p (j t) -> p j t", t=P)
        mask = lay2[:, nsel:nsel + 4 * P].rearrange("p (j t) -> p j t", t=P)
        f3s = lay2[:, nsel + 4 * P:nsel + 4 * P + nf].rearrange("p (k n) -> p k n", k=KD)
        f23 = lay2[:, nsel + 4 * P + nf:nsel + 4 * P + 2 * nf].rearrange("p (k n) -> p k n", k=KD)
        brow = sb("brow", [LO + 1, FB])
        bias_r = sb("bias_r", [LO + 1, FB], F32R)
        ones_r = sb("ones_r", [LO + 1, P], F32R)
        wo = sb("wo", [P, KI, D])
        rmsw = sb("rmsw", [P, KI])
        cw = sb("cw", [P, CT, TAPS])
        cb = sb("cb", [P, CT])
        a_neg = sb("a_neg", [P, H])
        d_bc = sb("d_bc", [P, H])
        lng = sb("lng", [P, D])
        lnb = sb("lnb", [P, D])
        ident = sb("ident", [P, P])
        ident_r = sb("ident_r", [P, P], F32R)
        ones = sb("ones", [P, P])
        upto = sb("upto", [P, P])
        after = sb("after", [P, P])
        mask_r = sb("mask_r", [P, 4 * P], F32R)
        sel_r = sb("sel_r", [LO + 2 * H, 2 * H, P], F32R)
        nhalf = sb("nhalf", [P, 2])

        xin = sb("xin", [P, BUF, Q, D])
        xn = sb("xn", [P, BUF, Q, D])
        raw = sb("raw", [P, BUF, CT, Q, HALO + P])
        xs = sb("xs", [P, BUF, CT, Q, P])
        gate = sb("gate", [P, BUF, Q, DI])
        res = sb("res", [P, BUF, Q, D])
        dts = sb("dts", [P, BUF, Q * H])
        exs = sb("exs", [P, BUF, 3 * Q * H])
        obuf = sb("obuf", [P, BUF, Q, D])
        xh = sb("xh", [P, KD, Q, P], F32R)
        xl = sb("xl", [P, KD, Q, P], F32R)
        u = sb("u", [P, CT, Q, P])
        ft = sb("ft", [P, Q, D])
        st1 = sb("st1", [P, Q, 6])
        mv1 = sb("mv1", [P, Q, 2])
        ve1 = sb("ve1", [P, Q])
        rs1 = sb("rs1", [P, Q])
        v16 = sb("v16", [P, Q, H])
        m2 = sb("m2", [P, Q * H])
        nab = sb("nab", [P, Q * H])
        ee = sb("ee", [P, Q * H])
        den = sb("den", [P, Q * H])
        rc = sb("rc", [P, Q * H])
        sv = sb("sv", [P, Q * H])
        ww = sb("ww", [P, Q * H])
        pa = sb("pa", [P, Q * H])
        pb = sb("pb", [P, Q * H])
        a48 = sb("a48", [P, LO + Q * H])
        w16 = sb("w16", [P, Q * H])
        ncs = sb("ncs", [P, Q * H])
        rows = sb("rows", [LO + Q * H, P], F32R)
        xsb = sb("xsb", [P, Q, DI])
        xdt = sb("xdt", [P, Q, DI])
        xw = sb("xw", [P, Q, DI])
        xd = sb("xd", [P, Q, DI])
        btg = sb("btg", [P, Q, 2 * P])
        el, mm = (lay1[:, i * Q * H * P:(i + 1) * Q * H * P].rearrange("p (q h t) -> p q h t", q=Q, h=H)
                  for i in range(2))
        state = sb("state", [P, Q, DI])
        sdec = sb("sdec", [P, Q, DI])
        t1, t2, y, yg = (lay2[:, i * Q * DI:(i + 1) * Q * DI].rearrange("p (q n) -> p q n", q=Q) for i in range(4))
        junk = sb("junk", [P, DI])
        ss = sb("ss", [P, Q])
        sse = sb("sse", [P, Q])
        rr = sb("rr", [P, Q])
        yts = sb("yts", [P, Q, KI, P])
        hh = sb("hh", [P, Q, D])
        st2 = sb("st2", [P, Q, 6])
        mv2 = sb("mv2", [P, Q, 2])
        ve2 = sb("ve2", [P, Q])
        rs2 = sb("rs2", [P, Q])

        s_load = sem("s_load")
        s_gp = sem("s_gp")
        s_const = sem("s_const")
        s_dv = sem("s_dv")
        s_split = sem("s_split")
        s_f23 = sem("s_f23")
        s_f23s = sem("s_f23s")
        s_f123 = sem("s_f123")
        s_an = sem("s_an")
        s_apart = sem("s_apart")
        x_loaded = sems("x_loaded", BUF)
        stored = sems("stored", BUF)
        st1_done, mv1_done, ve1_done, rs1_done, xn_done = map(sem, ("st1_done", "mv1_done", "ve1_done", "rs1_done", "xn_done"))
        xt_in_psum, xh_done, xl_done = map(sem, ("xt_in_psum", "xh_done", "xl_done"))
        f_in_psum, f_read, z_in_psum, zt_done, gate_done = (sems(n, Q) for n in ("f_in_psum", "f_read", "z_in_psum", "zt_done", "gate_done"))
        c_in_psum, raw_done, th_done, xs_done = (sems(n, NG) for n in ("c_in_psum", "raw_done", "th_done", "xs_done"))
        tap_done = [sems(f"tap_done{t}_", NG) for t in range(TAPS)]
        halo_done, m2_done, nab_done, ee_done, den_done, rc_done = map(sem, ("halo_done", "m2_done", "nab_done", "ee_done", "den_done", "rc_done"))
        log_chain, a_done, res_chain, res_done = map(sem, ("log_chain", "a_done", "res_chain", "res_done"))
        sums_in_psum, sums_read, rows_done, w16_done = map(sem, ("sums_in_psum", "sums_read", "rows_done", "w16_done"))
        (xt2_in_psum, xsb_done, xdt_done, xw_done, xd_done, sdec_done, bg_in_psum, bg_read, yoff_in_psum, t1_done,
         t2_done, st_in_psum, state_done, yd_in_psum, y_done, yg_done, ss_done, sse_done, rr_done, yt_in_psum, yts_done,
         o_in_psum, h_done, st2_done, mv2_done, ve2_done, rs2_done, hn_done, hg_done, out_done) = (
            sems(n, Q) for n in (
                "xt2_in_psum", "xsb_done", "xdt_done", "xw_done", "xd_done", "sdec_done", "bg_in_psum", "bg_read",
                "yoff_in_psum", "t1_done", "t2_done", "st_in_psum", "state_done", "yd_in_psum", "y_done", "yg_done",
                "ss_done", "sse_done", "rr_done", "yt_in_psum", "yts_done", "o_in_psum", "h_done", "st2_done",
                "mv2_done", "ve2_done", "rs2_done", "hn_done", "hg_done", "out_done"))
        e_in_psum, e_done, m_done = ([sems(f"{n}{q}_", 2) for q in range(Q)] for n in ("e_in_psum", "e_done", "m_done"))

        def after_step(eng, event, step):
            if isinstance(step, int) and step < 0:
                return
            eng.wait_ge(event, step + 1)

        def apart(eng):
            eng.sem_inc(s_apart, 1)

        def passes(eng, one_pass):
            for k in range(-2, BUF):
                one_pass(k, k % BUF, k + 2 < steps, k >= -1, k >= 0)
            full = (steps - 2) // BUF
            with eng.Fori(1, full) as i:
                for b in range(BUF):
                    one_pass(i * BUF + b, b, True, True, True)
            for k in range(full * BUF, steps):
                one_pass(k, k % BUF, k + 2 < steps, k + 1 < steps, True)

        def heads(ap):
            return ap.rearrange("p (h c) -> p h c", h=H)

        def per_head(ap):
            return ap.unsqueeze(2).to_broadcast([P, H, HD])

        def count16(k, b):
            if isinstance(k, int):
                return 16 * (k // BUF + 1)
            return (k - b) // BUF * 16 + 16

        block = ctx.enter_context(nc.Block())

        @block.sync
        def _(sp):
            def load(step, b, rows_at):
                sp.dma_start(xin[:, b], x_t[rows_at, :, :]).then_inc(x_loaded[b], 16)

            for j in range(BUF):
                load(j, j, slice(j * P, (j + 1) * P))
            loads = [
                (win[:, :, :], w_in.rearrange("(k p) n -> p k n", p=P)),
                (f1s[:, :, :], f1t.rearrange("(k p) n -> p k n", p=P)),
                (f2s[:, :, :], f2t.rearrange("(k p) n -> p k n", p=P)),
                (f3s[:, :, :], f3.rearrange("(k p) n -> p k n", p=P)),
                (wo[:, :, :], w_out.rearrange("(k p) n -> p k n", p=P)),
                (rmsw[:, :], rms_w), (cw[:, :, :], conv_w.rearrange("(k p) n -> p k n", p=P)), (cb[:, :], conv_b),
                (a_neg[:, :], a_log.partition_broadcast(P)), (d_bc[:, :], d_skip.partition_broadcast(P)),
                (lng[:, :], ln_g.partition_broadcast(P)), (lnb[:, :], ln_b.partition_broadcast(P)),
            ]
            for dst, src in loads:
                sp.dma_start(dst, src).then_inc(s_load, 16)
            sp.wait_ge(s_gp, 1)
            for row in (0, LO):
                sp.dma_start(brow[row:row + 1, 0:D], f_bias.rearrange("(a n) -> a n", a=1)).then_inc(s_load, 16)
                sp.dma_start(brow[row:row + 1, D:FB], dt_bias.rearrange("(a n) -> a n", a=1)).then_inc(s_load, 16)

            def one_pass(k, b, has_l, has_f, has_s):
                if has_f and (not isinstance(k, int) or k + 1 + BUF < steps):
                    after_step(sp, res_done, k + 1)
                    nb = (b + 1) % BUF
                    load(k + 4, nb, bass.ds((k + 1 + BUF) * P, P) if not isinstance(k, int)
                         else slice((k + 1 + BUF) * P, (k + 2 + BUF) * P))
                if has_s:
                    after_step(sp, out_done[0], k)
                    after_step(sp, out_done[1], k)
                    at = slice(k * P, (k + 1) * P) if isinstance(k, int) else bass.ds(k * P, P)
                    sp.dma_start(out_t[at, :, :], obuf[:, b]).then_inc(stored[b], 16)

            for k in range(-2, BUF):
                one_pass(k, k % BUF, True, k >= -1, k >= 0)
            full = (steps - 1 - BUF) // BUF
            with sp.Fori(1, full) as i:
                for b in range(BUF):
                    one_pass(i * BUF + b, b, True, True, True)
            for k in range(full * BUF, steps):
                one_pass(k, k % BUF, k + 2 < steps, k + 1 < steps, True)
            for b in range(BUF):
                sp.wait_ge(stored[b], 16 * len(range(b, steps, BUF)))

        n_loads = 12 + 4

        @block.gpsimd
        def _(pool):
            g = nc.gpsimd
            g.memset(brow[:, :], 0.0).then_inc(s_gp, 1)
            g.memset(ident[:, :], 0.0).then_inc(s_gp, 1)
            g.memset(ones[:, :], 1.0).then_inc(s_gp, 1)
            g.memset(mask[:, :, :], 0.0).then_inc(s_gp, 1)
            g.memset(sel[:, :, :], 0.0).then_inc(s_gp, 1)
            g.memset(nhalf[:, :], -0.5).then_inc(s_gp, 1)
            g.memset(a48[:, :], 0.0).then_inc(s_gp, 1)
            g.memset(state[:, :, :], 0.0).then_inc(s_gp, 1)
            g.memset(raw[:, 0, :, :, 0:HALO], 0.0).then_inc(halo_done, 1)
            pool.wait_ge(s_gp, 8)
            g.affine_select(out=ident[:, :], in_=ident[:, :], compare_op=ALU.not_equal, fill=1.0, base=0,
                            pattern=[[-1, P]], channel_multiplier=1).then_inc(s_gp, 1)
            g.affine_select(out=upto[:, :], in_=ones[:, :], compare_op=ALU.is_ge, fill=0.0, base=0,
                            pattern=[[1, P]], channel_multiplier=-1).then_inc(s_gp, 1)
            g.affine_select(out=after[:, :], in_=ones[:, :], compare_op=ALU.is_gt, fill=0.0, base=0,
                            pattern=[[-1, P]], channel_multiplier=1).then_inc(s_gp, 1)
            g.affine_select(out=mask[:, :, :], in_=mask[:, :, :], compare_op=ALU.is_ge, fill=BIG, base=0,
                            pattern=[[0, 4], [1, P]], channel_multiplier=-1).then_inc(s_gp, 1)
            g.affine_select(out=sel[:, :, :], in_=sel[:, :, :], compare_op=ALU.not_equal, fill=1.0, base=0,
                            pattern=[[-1, Q * H], [0, P]], channel_multiplier=1).then_inc(s_gp, 1)
            pool.wait_ge(s_gp, 13)
            g.affine_select(out=sel[:, :, :], in_=sel[:, :, :], compare_op=ALU.not_equal, fill=1.0, base=-LO,
                            pattern=[[-1, Q * H], [0, P]], channel_multiplier=1).then_inc(s_const, 1)
            pool.wait_ge(s_load, 16 * n_loads)
            pool.wait_ge(s_split, 1)

            def layer_norm_scale(k):
                after_step(pool, mv1_done, k)
                apart(pool)
                g.tensor_scalar(ve1[:, :], mv1[:, :, 1], EPS, 1.0, ALU.add, ALU.mult).then_inc(ve1_done, 1)
                after_step(pool, ve1_done, k)
                g.tensor_tensor(rs1[:, :], ve1[:, :], nhalf[:, :], ALU.pow).then_inc(rs1_done, 1)

            def halo(k, b):
                for c in range(NG):
                    after_step(pool, raw_done[c], k - 1)
                pb_ = (b - 1) % BUF
                if not isinstance(k, int) or k > 0:
                    apart(pool)
                    g.tensor_copy(raw[:, b, :, :, 0:HALO], raw[:, pb_, :, :, P:P + HALO]).then_inc(halo_done, 1)

            def softplus_in(k):
                after_step(pool, f_read[0], k)
                after_step(pool, f_read[1], k)
                v = v16[:, :, :].rearrange("p q h -> p (q h)")
                apart(pool)
                g.tensor_scalar(m2[:, :], v, 0.0, -2.0, ALU.max, ALU.mult).then_inc(m2_done, 1)
                after_step(pool, m2_done, k)
                g.tensor_tensor(nab[:, :], v, m2[:, :], ALU.add).then_inc(nab_done, 1)

            def softplus_den(k):
                after_step(pool, ee_done, k)
                apart(pool)
                g.tensor_scalar(den[:, :], ee[:, :], 2.0, 1.0, ALU.add, ALU.mult).then_inc(den_done, 1)

            CH = 2 * LOG_TERMS + 2

            def softplus_out(k, b):
                after_step(pool, rc_done, k)
                n = [0]

                def link(ins):
                    n[0] += 1
                    ins.then_inc(log_chain, 1)
                    pool.wait_ge(log_chain, k * CH + n[0])

                link(g.tensor_tensor(sv[:, :], ee[:, :], rc[:, :], ALU.mult))
                link(g.tensor_tensor(ww[:, :], sv[:, :], sv[:, :], ALU.mult))
                apart(pool)
                link(g.tensor_scalar(pa[:, :], ww[:, :], logc[-1], logc[-2], ALU.mult, ALU.add))
                for c in logc[-3::-1]:
                    link(g.tensor_tensor(pb[:, :], pa[:, :], ww[:, :], ALU.mult))
                    apart(pool)
                    link(g.tensor_scalar(pa[:, :], pb[:, :], c, 1.0, ALU.add, ALU.mult))
                link(g.tensor_tensor(pb[:, :], pa[:, :], sv[:, :], ALU.mult))
                apart(pool)
                link(g.tensor_scalar(m2[:, :], m2[:, :], -0.5, 0.0, ALU.mult, ALU.add))
                link(g.tensor_tensor(dts[:, b], pb[:, :], m2[:, :], ALU.add))
                assert n[0] == CH
                d3 = dts[:, b].rearrange("p (q h) -> p q h", q=Q)
                a3 = a_neg[:, :].unsqueeze(1).to_broadcast([P, Q, H])
                for at in (0, LO):
                    ins = g.tensor_tensor(a48[:, at:at + Q * H].rearrange("p (q h) -> p q h", q=Q), d3, a3, ALU.mult)
                ins.then_inc(a_done, 1)

            def residual(k, b):
                g.tensor_tensor(res[:, b], xin[:, b], ft[:, :, :], ALU.add).then_inc(res_chain, 1)
                after_step(pool, res_chain, k)
                g.tensor_tensor(res[:, b], res[:, b], lnb[:, :].unsqueeze(1).to_broadcast([P, Q, D]), ALU.add)\
                    .then_inc(res_done, 1)

            def state_weights(k, b):
                after_step(pool, sums_read, k)
                g.tensor_tensor(w16[:, :], dts[:, b], exs[:, b, Q * H:2 * Q * H], ALU.mult).then_inc(w16_done, 1)

            def scale_x(k, b, q):
                after_step(pool, xsb_done[q], k)
                if q == 0:
                    after_step(pool, w16_done, k)
                g.tensor_tensor(heads(xw[:, q]), heads(xsb[:, q]), per_head(w16[:, q * H:(q + 1) * H]), ALU.mult)\
                    .then_inc(xw_done[q], 1)
                after_step(pool, state_done[q], k - 1)
                g.tensor_tensor(heads(sdec[:, q]), heads(state[:, q]),
                                per_head(exs[:, b, 2 * Q * H + q * H:2 * Q * H + (q + 1) * H]), ALU.mult)\
                    .then_inc(sdec_done[q], 1)
                g.tensor_tensor(heads(xd[:, q]), heads(xsb[:, q]), per_head(d_bc[:, :]), ALU.mult)\
                    .then_inc(xd_done[q], 1)

            def add_skip(k, q):
                after_step(pool, t1_done[q], k)
                after_step(pool, xd_done[q], k)
                g.tensor_tensor(t2[:, q], t1[:, q], xd[:, q], ALU.add).then_inc(t2_done[q], 1)

            def rms_scale(k, q):
                after_step(pool, ss_done[q], k)
                apart(pool)
                g.tensor_scalar(sse[:, q:q + 1], ss[:, q:q + 1], 1.0 / DI, EPS, ALU.mult, ALU.add).then_inc(sse_done[q], 1)
                after_step(pool, sse_done[q], k)
                g.tensor_tensor(rr[:, q:q + 1], sse[:, q:q + 1], nhalf[:, 0:1], ALU.pow).then_inc(rr_done[q], 1)

            def last_norm_scale(k, q):
                after_step(pool, mv2_done[q], k)
                apart(pool)
                g.tensor_scalar(ve2[:, q:q + 1], mv2[:, q, 1:2], EPS, 1.0, ALU.add, ALU.mult).then_inc(ve2_done[q], 1)
                after_step(pool, ve2_done[q], k)
                g.tensor_tensor(rs2[:, q:q + 1], ve2[:, q:q + 1], nhalf[:, 0:1], ALU.pow).then_inc(rs2_done[q], 1)

            def output(k, b, q):
                after_step(pool, hn_done[q], k)
                if not isinstance(k, int) or k >= BUF:
                    if q == 0:
                        pool.wait_ge(stored[b], count16(k - BUF, b))
                g.tensor_tensor(obuf[:, b, q], hh[:, q], lng[:, :], ALU.mult).then_inc(hg_done[q], 1)
                after_step(pool, hg_done[q], k)
                g.tensor_tensor(obuf[:, b, q], obuf[:, b, q], res[:, b, q], ALU.add).then_inc(out_done[q], 1)

            def one_pass(k, b, has_l, has_f, has_s):
                b1 = (b + 1) % BUF
                if has_f:
                    halo(k + 1, b1)
                if has_s:
                    state_weights(k, b)
                    scale_x(k, b, 0)
                if has_f:
                    softplus_in(k + 1)
                if has_s:
                    add_skip(k, 0)
                if has_l:
                    layer_norm_scale(k + 2)
                if has_f:
                    softplus_den(k + 1)
                if has_s:
                    scale_x(k, b, 1)
                if has_f:
                    softplus_out(k + 1, b1)
                    residual(k + 1, b1)
                if has_s:
                    rms_scale(k, 0)
                    add_skip(k, 1)
                    last_norm_scale(k, 0)
                    rms_scale(k, 1)
                    output(k, b, 0)
                    last_norm_scale(k, 1)
                    output(k, b, 1)

            passes(pool, one_pass)

        @block.vector
        def _(dve):
            v = nc.vector
            dve.wait_ge(s_load, 16 * n_loads)
            dve.wait_ge(s_an, 1)
            v.tensor_scalar(a_neg[:, :], a_neg[:, :], -1.0, None, ALU.mult).then_inc(s_split, 1)
            parts = [(win[:, :, 0:DI], ZC, DI, 0.5), (win[:, :, DI:DI + CONV], CC, CONV, 1.0),
                     (win[:, :, DI + CONV:DI + CONV + H], FC + D, H, 1.0)]
            for src, at, n, scale in parts:
                v.tensor_scalar(wh[:, :, at:at + n], src, scale, None, ALU.mult).then_inc(s_dv, 1)
            v.tensor_copy(bias_r[:, :], brow[:, :]).then_inc(s_dv, 1)
            dve.wait_ge(s_const, 1)
            v.tensor_copy(ident_r[:, :], ident[:, :])
            v.tensor_copy(mask_r[:, :], mask[:, :, :].rearrange("p a t -> p (a t)"))
            v.tensor_copy(sel_r[:, :, :], sel[:, :, :])
            v.tensor_copy(ones_r[:, :], ones[0:LO + 1, :])
            dve.wait_ge(s_dv, 4)
            for src, at, n, scale in parts:
                for kd in range(KD):
                    v.scalar_tensor_tensor(out=wl[:, kd, at:at + n], in0=src[:, kd], scalar=scale,
                                           in1=wh[:, kd, at:at + n].bitcast(F32), op0=ALU.mult, op1=ALU.subtract)
            v.tensor_tensor(bias_r[LO:LO + 1, :], brow[LO:LO + 1, :], bias_r[LO:LO + 1, :].bitcast(F32), ALU.subtract)
            for ki in range(KI):
                v.tensor_scalar(wo[:, ki], wo[:, ki], rmsw[:, ki:ki + 1], None, ALU.mult)
            v.tensor_scalar(cw[:, :, :], cw[:, :, :], 0.5, None, ALU.mult)
            v.tensor_scalar(cb[:, :], cb[:, :], 0.5, None, ALU.mult)
            for m, bank in enumerate((ring0, ring1)):
                dve.wait_ge(s_f23, m + 1)
                v.tensor_copy(f23[:, m, :], bank[:, 0:D]).then_inc(s_f23s, 1)
            for m, bank in enumerate((ring0, ring1)):
                dve.wait_ge(s_f123, m + 1)
                v.tensor_copy(wh[:, m, FC:FC + D], bank[:, 0:D]).then_inc(s_dv, 1)
            for m, bank in enumerate((ring0, ring1)):
                dve.wait_ge(s_dv, 5 + m)
                last = v.tensor_tensor(wl[:, m, FC:FC + D], bank[:, 0:D], wh[:, m, FC:FC + D].bitcast(F32), ALU.subtract)
            last.then_inc(s_split, 1)
            dve.wait_ge(s_split, 2)

            def norm_stats(k, b):
                dve.wait_ge(x_loaded[b], count16(k, b))
                for q in range(Q):
                    last = v.bn_stats(st1[:, q], xin[:, b, q])
                last.then_inc(st1_done, 1)
                after_step(dve, st1_done, k)
                apart(dve)
                for q in range(Q):
                    last = v.bn_aggr(mv1[:, q], st1[:, q])
                last.then_inc(mv1_done, 1)

            def norm_apply(k, b):
                after_step(dve, rs1_done, k)
                for q in range(Q):
                    last = v.tensor_scalar(xn[:, b, q], xin[:, b, q], mv1[:, q, 0:1], rs1[:, q:q + 1],
                                           ALU.subtract, ALU.mult)
                last.then_inc(xn_done, 1)

            def low_part(k):
                after_step(dve, xh_done, k)
                v.tensor_tensor(xl[:, :, :, :].rearrange("p k q t -> p (k q t)"), ring1[:, :],
                                xh[:, :, :, :].rearrange("p k q t -> p (k q t)").bitcast(F32), ALU.subtract)\
                    .then_inc(xl_done, 1)

            def tap(k, b, t):
                for c in range(NG):
                    if t == 0:
                        after_step(dve, raw_done[c], k)
                        if c == 0:
                            after_step(dve, halo_done, k)
                    else:
                        after_step(dve, tap_done[t - 1][c], k)
                    for ct in (2 * c, 2 * c + 1):
                        src = raw[:, b, ct, :, t:t + P]
                        if t == 0:
                            last = v.tensor_scalar(u[:, ct], src, cw[:, ct, 0:1], cb[:, ct:ct + 1], ALU.mult, ALU.add)
                        else:
                            last = v.scalar_tensor_tensor(out=u[:, ct], in0=src, scalar=cw[:, ct, t:t + 1], in1=u[:, ct],
                                                          op0=ALU.mult, op1=ALU.add)
                    last.then_inc(tap_done[t][c], 1)

            def silu(k, b, c):
                after_step(dve, th_done[c], k)
                part = slice(2 * c, 2 * c + 2)
                v.scalar_tensor_tensor(out=xs[:, b, part].rearrange("p c q t -> p (c q t)"),
                                       in0=xs[:, b, part].rearrange("p c q t -> p (c q t)"), scalar=1.0,
                                       in1=u[:, part].rearrange("p c q t -> p (c q t)"),
                                       op0=ALU.add, op1=ALU.mult).then_inc(xs_done[c], 1)

            def gates(k, b, q):
                after_step(dve, zt_done[q], k)
                bank = (ring1, ring0)[q]
                v.scalar_tensor_tensor(out=gate[:, b, q], in0=gate[:, b, q], scalar=1.0, in1=bank[:, :],
                                       op0=ALU.add, op1=ALU.mult).then_inc(gate_done[q], 1)

            def softplus_rec(k):
                after_step(dve, den_done, k)
                v.reciprocal(rc[:, :], den[:, :]).then_inc(rc_done, 1)

            def low_rows(k):
                after_step(dve, sums_read, k)
                v.tensor_tensor(rows[LO:LO + Q * H, :], bg_bank[LO:LO + Q * H, 64:64 + P],
                                rows[LO:LO + Q * H, :].bitcast(F32), ALU.subtract).then_inc(rows_done, 1)

            def x_times_dt(k, b, q):
                after_step(dve, xsb_done[q], k)
                v.tensor_tensor(heads(xdt[:, q]), heads(xsb[:, q]), per_head(dts[:, b, q * H:(q + 1) * H]), ALU.mult)\
                    .then_inc(xdt_done[q], 1)

            def weigh(k, q, half):
                after_step(dve, e_done[q][half], k)
                if half == 0:
                    after_step(dve, bg_read[q], k)
                hs = slice(4 * half, 4 * half + 4)
                v.tensor_tensor(mm[:, q, hs], el[:, q, hs], btg[:, q, P:2 * P].unsqueeze(1).to_broadcast([P, 4, P]),
                                ALU.mult).then_inc(m_done[q][half], 1)

            def scale_off(k, b, q):
                after_step(dve, yoff_in_psum[q], k)
                v.tensor_tensor(heads(t1[:, q]), heads(yoff_bank[:, :]), per_head(exs[:, b, q * H:(q + 1) * H]), ALU.mult)\
                    .then_inc(t1_done[q], 1)

            def new_state(k, q):
                after_step(dve, st_in_psum[q], k)
                after_step(dve, sdec_done[q], k)
                v.tensor_tensor(state[:, q], xt_bank[:, :], sdec[:, q], ALU.add).then_inc(state_done[q], 1)

            def add_diag(k, q):
                after_step(dve, yd_in_psum[q], k)
                after_step(dve, t2_done[q], k)
                v.tensor_tensor(y[:, q], yd_bank[:, :], t2[:, q], ALU.add).then_inc(y_done[q], 1)

            def apply_gate(k, b, q):
                after_step(dve, y_done[q], k)
                v.tensor_tensor(yg[:, q], y[:, q], gate[:, b, q], ALU.mult).then_inc(yg_done[q], 1)

            def last_h(k, b, q):
                after_step(dve, o_in_psum[q], k)
                after_step(dve, rr_done[q], k)
                bank = (ring0, ring1)[q]
                v.scalar_tensor_tensor(out=hh[:, q], in0=bank[:, 0:D], scalar=rr[:, q:q + 1], in1=xn[:, b, q],
                                       op0=ALU.mult, op1=ALU.add).then_inc(h_done[q], 1)

            def last_stats(k, q):
                after_step(dve, h_done[q], k)
                v.bn_stats(st2[:, q], hh[:, q]).then_inc(st2_done[q], 1)
                after_step(dve, st2_done[q], k)
                apart(dve)
                v.bn_aggr(mv2[:, q], st2[:, q]).then_inc(mv2_done[q], 1)

            def last_apply(k, q):
                after_step(dve, rs2_done[q], k)
                v.tensor_scalar(hh[:, q], hh[:, q], mv2[:, q, 0:1], rs2[:, q:q + 1], ALU.subtract, ALU.mult)\
                    .then_inc(hn_done[q], 1)

            def one_pass(k, b, has_l, has_f, has_s):
                b1, b2 = (b + 1) % BUF, (b + 2) % BUF
                if has_s:
                    low_rows(k)
                if has_l:
                    norm_stats(k + 2, b2)
                if has_s:
                    x_times_dt(k, b, 0)
                    weigh(k, 0, 0)
                    weigh(k, 0, 1)
                if has_f:
                    tap(k + 1, b1, 0)
                if has_s:
                    scale_off(k, b, 0)
                    new_state(k, 0)
                if has_f:
                    tap(k + 1, b1, 1)
                if has_l:
                    norm_apply(k + 2, b2)
                if has_s:
                    add_diag(k, 0)
                if has_f:
                    tap(k + 1, b1, 2)
                if has_s:
                    apply_gate(k, b, 0)
                    x_times_dt(k, b, 1)
                    weigh(k, 1, 0)
                    weigh(k, 1, 1)
                if has_f:
                    tap(k + 1, b1, 3)
                    softplus_rec(k + 1)
                if has_s:
                    scale_off(k, b, 1)
                    new_state(k, 1)
                if has_f:
                    for c in range(NG):
                        silu(k + 1, b1, c)
                    gates(k + 1, b1, 0)
                    gates(k + 1, b1, 1)
                if has_s:
                    add_diag(k, 1)
                    last_h(k, b, 0)
                    apply_gate(k, b, 1)
                    last_stats(k, 0)
                if has_l:
                    low_part(k + 2)
                if has_s:
                    last_apply(k, 0)
                    last_h(k, b, 1)
                    last_stats(k, 1)
                    last_apply(k, 1)

            passes(dve, one_pass)

        @block.scalar
        def _(act):
            s = nc.scalar
            act.wait_ge(s_load, 16 * n_loads)
            s.activation(a_neg[:, :], a_neg[:, :], ACT.Exp).then_inc(s_an, 1)
            act.wait_ge(s_split, 2)

            def high_part(k):
                after_step(act, xt_in_psum, k)
                s.activation(xh[:, :, :, :].rearrange("p k q t -> p (k q t)"), ring1[:, :], ACT.Copy).then_inc(xh_done, 1)

            def branch(k, q):
                after_step(act, f_in_psum[q], k)
                bank = (ring0, ring1)[q]
                if q == 0:
                    after_step(act, res_chain, k - 1)
                s.activation(ft[:, q], bank[:, 0:D], ACT.Tanh)
                s.activation(v16[:, q], bank[:, D:FB], ACT.Copy).then_inc(f_read[q], 1)

            def conv_in(k, b, c):
                after_step(act, c_in_psum[c], k)
                bank = (ring0, ring1, ring0)[c]
                s.activation(raw[:, b, 2 * c:2 * c + 2, :, HALO:], bank[:, :].rearrange("p (c q t) -> p c q t", c=2, q=Q),
                             ACT.Copy).then_inc(raw_done[c], 1)

            def softplus_exp(k):
                after_step(act, nab_done, k)
                s.activation(ee[:, :], nab[:, :], ACT.Exp).then_inc(ee_done, 1)

            def conv_tanh(k, b, c):
                after_step(act, tap_done[TAPS - 1][c], k)
                part = slice(2 * c, 2 * c + 2)
                s.activation(xs[:, b, part], u[:, part], ACT.Tanh).then_inc(th_done[c], 1)

            def z_tanh(k, b, q):
                after_step(act, z_in_psum[q], k)
                bank = (ring1, ring0)[q]
                s.activation(gate[:, b, q], bank[:, :], ACT.Tanh).then_inc(zt_done[q], 1)

            def sums(k, b):
                after_step(act, sums_in_psum, k)
                s.activation(exs[:, b], bg_bank[:, 0:3 * Q * H], ACT.Exp)
                s.mul(ncs[:, :], bg_bank[:, 0:Q * H], -1.0)
                s.activation(rows[:, :], bg_bank[0:LO + Q * H, 64:64 + P], ACT.Copy).then_inc(sums_read, 1)

            def x_tokens(k, q):
                after_step(act, xt2_in_psum[q], k)
                s.activation(xsb[:, q], xt_bank[:, :], ACT.Copy).then_inc(xsb_done[q], 1)

            def b_and_g(k, q):
                after_step(act, bg_in_psum[q], k)
                s.activation(btg[:, q], bg_bank[:, 0:2 * P], ACT.Copy).then_inc(bg_read[q], 1)

            def decay(k, q, half):
                after_step(act, e_in_psum[q][half], k)
                after_step(act, m_done[q][half], k - 1)
                if q == 0 and half == 0:
                    after_step(act, sums_read, k)
                for j in range(4):
                    h = 4 * half + j
                    last = s.activation(el[:, q, h], e_bank[half][:, j * P:(j + 1) * P], ACT.Exp,
                                        bias=ncs[:, q * H + h:q * H + h + 1])
                last.then_inc(e_done[q][half], 1)

            def square(k, q):
                after_step(act, yg_done[q], k)
                s.activation(junk[:, :], yg[:, q], ACT.Square, accum_out=ss[:, q:q + 1]).then_inc(ss_done[q], 1)

            def y_channels(k, q):
                after_step(act, yt_in_psum[q], k)
                s.activation(yts[:, q].rearrange("p k t -> p (k t)"), yd_bank[:, :], ACT.Copy).then_inc(yts_done[q], 1)

            def one_pass(k, b, has_l, has_f, has_s):
                b1 = (b + 1) % BUF
                if has_s:
                    sums(k, b)
                    x_tokens(k, 0)
                    b_and_g(k, 0)
                    decay(k, 0, 0)
                    decay(k, 0, 1)
                if has_f:
                    branch(k + 1, 0)
                    branch(k + 1, 1)
                    for c in range(NG):
                        conv_in(k + 1, b1, c)
                    softplus_exp(k + 1)
                if has_s:
                    x_tokens(k, 1)
                    b_and_g(k, 1)
                    decay(k, 1, 0)
                    decay(k, 1, 1)
                if has_f:
                    z_tanh(k + 1, b1, 0)
                if has_s:
                    square(k, 0)
                    y_channels(k, 0)
                if has_f:
                    for c in range(NG):
                        conv_tanh(k + 1, b1, c)
                    z_tanh(k + 1, b1, 1)
                if has_l:
                    high_part(k + 2)
                if has_s:
                    square(k, 1)
                    y_channels(k, 1)

            passes(act, one_pass)

        @block.tensor
        def _(pe):
            mul, tr = nc.tensor.matmul, nc.tensor.transpose
            pe.wait_ge(s_load, 16 * n_loads)
            for m, bank in enumerate((ring0, ring1)):
                for kd in range(KD):
                    last = mul(bank[:, 0:D], f2s[:, kd, m * P:(m + 1) * P], f3s[:, kd], start=kd == 0, stop=kd == KD - 1)
                last.then_inc(s_f23, 1)
            pe.wait_ge(s_f23s, KD)
            for m, bank in enumerate((ring0, ring1)):
                for kd in range(KD):
                    last = mul(bank[:, 0:D], f1s[:, kd, m * P:(m + 1) * P], f23[:, kd], start=kd == 0, stop=kd == KD - 1)
                last.then_inc(s_f123, 1)
            pe.wait_ge(s_split, 2)

            def transpose_x(k, b):
                after_step(pe, xn_done, k)
                after_step(pe, gate_done[0], k - 1)
                for kd in range(KD):
                    for q in range(Q):
                        at = (kd * Q + q) * P
                        last = tr(ring1[:, at:at + P], xn[:, b, q, kd * P:(kd + 1) * P], ident[:, :])
                last.then_inc(xt_in_psum, 1)

            def split_products(out, pairs, first=True):
                n = len(pairs)
                for i, (a, c) in enumerate(pairs):
                    last = mul(out, a, c, start=first and i == 0, stop=i == n - 1)
                return last

            def conv_project(k, c):
                if c == 0:
                    after_step(pe, f_read[0], k)
                elif c == 1:
                    after_step(pe, f_read[1], k)
                else:
                    after_step(pe, raw_done[0], k)
                bank = (ring0, ring1, ring0)[c]
                for i, ct in enumerate((2 * c, 2 * c + 1)):
                    cols = slice(CC + ct * P, CC + (ct + 1) * P)
                    pairs = []
                    for kd in range(KD):
                        xh_, xl_ = (t[:, kd].rearrange("p q t -> p (q t)") for t in (xh, xl))
                        pairs += [(wh[:, kd, cols], xh_), (wh[:, kd, cols], xl_), (wl[:, kd, cols], xh_)]
                    last = split_products(bank[:, i * Q * P:(i + 1) * Q * P], pairs)
                last.then_inc(c_in_psum[c], 1)

            def z_project(k, q):
                after_step(pe, raw_done[1 + q], k)
                cols = slice(ZC, ZC + DI)
                pairs = []
                for kd in range(KD):
                    pairs += [(xh[:, kd, q], wh[:, kd, cols]), (xh[:, kd, q], wl[:, kd, cols]), (xl[:, kd, q], wh[:, kd, cols])]
                split_products((ring1, ring0)[q][:, :], pairs).then_inc(z_in_psum[q], 1)

            def branch_project(k, q):
                after_step(pe, xl_done, k)
                after_step(pe, h_done[q], k - 2)
                bank = (ring0, ring1)[q][:, 0:FB]
                mul(bank, ones_r[:, :], bias_r[:, :], start=True, stop=False)
                cols = slice(FC, FC + FB)
                pairs = []
                for kd in range(KD):
                    pairs += [(xh[:, kd, q], wh[:, kd, cols]), (xh[:, kd, q], wl[:, kd, cols]), (xl[:, kd, q], wh[:, kd, cols])]
                split_products(bank, pairs, first=False).then_inc(f_in_psum[q], 1)

            def sums(k):
                after_step(pe, a_done, k)
                after_step(pe, bg_read[1], k - 1)
                n = Q * H
                mul(bg_bank[:, 0:n], upto[:, :], a48[:, 0:n], start=True, stop=True)
                mul(bg_bank[:, n:2 * n], after[:, :], a48[:, 0:n], start=True, stop=True)
                mul(bg_bank[:, 2 * n:3 * n], ones[:, :], a48[:, 0:n], start=True, stop=True)
                mul(bg_bank[0:LO + n, 64:64 + P], a48[:, :], upto[:, :], start=True, stop=True).then_inc(sums_in_psum, 1)

            def x_tokens(k, b, q):
                after_step(pe, xs_done[NG - 1], k)
                after_step(pe, state_done[1 - q], k - 1 + q)
                for ct in range(KI):
                    last = tr(xt_bank[:, ct * P:(ct + 1) * P], xs[:, b, ct, q], ident[:, :])
                last.then_inc(xt2_in_psum[q], 1)

            def b_and_g(k, b, q):
                if q == 0:
                    after_step(pe, rows_done, k)
                else:
                    after_step(pe, bg_read[0], k)
                tr(bg_bank[:, 0:P], xs[:, b, KI, q], ident[:, :])
                mul(bg_bank[:, P:2 * P], xs[:, b, KI, q], xs[:, b, KI + 1, q], start=True, stop=True)\
                    .then_inc(bg_in_psum[q], 1)

            def exponents(k, q, half):
                if q == 0 and half == 0:
                    after_step(pe, rows_done, k)
                after_step(pe, e_done[1 - q][half], k - 1 + q)
                bank = e_bank[half]
                mul(bank[:, :], ident_r[:, :], mask_r[:, :], start=True, stop=False)
                for j in range(4):
                    last = mul(bank[:, j * P:(j + 1) * P], sel_r[:, q * H + 4 * half + j], rows[:, :], start=False, stop=j == 3)
                last.then_inc(e_in_psum[q][half], 1)

            def y_off(k, b, q):
                after_step(pe, t1_done[1 - q], k - 1 + q)
                after_step(pe, state_done[q], k - 1)
                mul(yoff_bank[:, :], xs[:, b, KI + 1, q], state[:, q], start=True, stop=True).then_inc(yoff_in_psum[q], 1)

            def states(k, q):
                after_step(pe, xsb_done[q], k)
                after_step(pe, xw_done[q], k)
                after_step(pe, bg_read[q], k)
                mul(xt_bank[:, :], btg[:, q, 0:P], xw[:, q], start=True, stop=True).then_inc(st_in_psum[q], 1)

            def y_diag(k, q):
                after_step(pe, yts_done[1 - q], k - 1 + q)
                after_step(pe, xdt_done[q], k)
                for h in range(H):
                    if h % 4 == 0:
                        after_step(pe, m_done[q][h // 4], k)
                    last = mul(yd_bank[:, h * HD:(h + 1) * HD], mm[:, q, h], xdt[:, q, h * HD:(h + 1) * HD],
                               start=True, stop=True)
                last.then_inc(yd_in_psum[q], 1)

            def transpose_y(k, q):
                after_step(pe, yg_done[q], k)
                for ki in range(KI):
                    last = tr(yd_bank[:, ki * P:(ki + 1) * P], yg[:, q, ki * P:(ki + 1) * P], ident[:, :])
                last.then_inc(yt_in_psum[q], 1)

            def out_project(k, q, has_l, has_f):
                after_step(pe, yts_done[q], k)
                if q == 0:
                    after_step(pe, gate_done[1], k + 1) if has_f else after_step(pe, h_done[0], k - 1)
                elif has_l:
                    after_step(pe, xl_done, k + 2)
                else:
                    after_step(pe, gate_done[0], k + 1) if has_f else after_step(pe, h_done[1], k - 1)
                bank = (ring0, ring1)[q]
                for ki in range(KI):
                    last = mul(bank[:, 0:D], yts[:, q, ki], wo[:, ki], start=ki == 0, stop=ki == KI - 1)
                last.then_inc(o_in_psum[q], 1)

            def one_pass(k, b, has_l, has_f, has_s):
                b1, b2 = (b + 1) % BUF, (b + 2) % BUF
                if has_s:
                    sums(k)
                    x_tokens(k, b, 0)
                if has_f:
                    branch_project(k + 1, 0)
                if has_s:
                    b_and_g(k, b, 0)
                    exponents(k, 0, 0)
                    exponents(k, 0, 1)
                if has_f:
                    branch_project(k + 1, 1)
                    conv_project(k + 1, 0)
                    conv_project(k + 1, 1)
                if has_s:
                    y_off(k, b, 0)
                    states(k, 0)
                    y_diag(k, 0)
                if has_f:
                    conv_project(k + 1, 2)
                if has_s:
                    x_tokens(k, b, 1)
                    b_and_g(k, b, 1)
                    exponents(k, 1, 0)
                    exponents(k, 1, 1)
                if has_f:
                    z_project(k + 1, 0)
                if has_s:
                    y_off(k, b, 1)
                    states(k, 1)
                    transpose_y(k, 0)
                if has_f:
                    z_project(k + 1, 1)
                if has_s:
                    y_diag(k, 1)
                    out_project(k, 0, has_l, has_f)
                if has_l:
                    transpose_x(k + 2, b2)
                if has_s:
                    transpose_y(k, 1)
                    out_project(k, 1, has_l, has_f)

            passes(pe, one_pass)


def kernel(**inputs):
    import numpy as _np
    import concourse.bacc as _bacc
    from concourse import mybir as _mybir
    from concourse.bass_utils import run_bass_kernel_spmd as _run

    a = {n: _np.asarray(v) for n, v in inputs.items()}
    laid_out = {
        "x": a["L0_attn_hidden_states"],
        "w_in": a["L0_attn_W_in"],
        "conv_w": a["L0_attn_conv_w"],
        "conv_b": a["L0_attn_conv_b"].reshape(-1, 128).T,
        "dt_bias": a["L0_attn_dt_bias"],
        "a_log": a["L0_attn_A_log"],
        "d_skip": a["L0_attn_D"],
        "rms_w": a["L0_attn_rms_w"].reshape(-1, 128).T,
        "w_out": a["L0_attn_W_out"],
        "ln_g": a["L0_attn_ln_g"],
        "ln_b": a["L0_attn_ln_b"],
        "f1t": a["L0_ffn_weight"].T,
        "f2t": a["L0_ffn_aux_weight1"].T,
        "f3": a["L0_ffn_aux_weight2"],
        "f_bias": a["L0_ffn_bias"],
    }
    nc = _bacc.Bacc("TRN2", target_bir_lowering=False, num_devices=1)
    arrays, args = {}, []
    for name, value in laid_out.items():
        value = _np.ascontiguousarray(value)
        arrays[f"in_{name}_dram"] = value
        args.append(nc.dram_tensor(f"in_{name}_dram", value.shape, _mybir.dt.from_np(value.dtype), kind="ExternalInput").ap())
    args.append(nc.dram_tensor("out_0_dram", laid_out["x"].shape, _mybir.dt.float32, kind="ExternalOutput").ap())
    program(nc, *args)
    r = _run(nc, [arrays], core_ids=[0])
    return r.results[0]["out_0_dram"]
```

```python
from contextlib import ExitStack

import numpy as np

import concourse.bass as bass
from concourse import mybir

F32 = mybir.dt.float32
F32R = mybir.dt.float32r
ALU = mybir.AluOpType
ACT = mybir.ActivationFunctionType
AXIS = mybir.AxisListType

P = 128
D = 256
DI = 512
H = 8
HD = DI // H
NS = 128
CONV = DI + 2 * NS
TAPS = 4
KD = D // P
KI = DI // P
CT = CONV // P
NG = CT // 2
Q = 2
HALO = TAPS - 1
EPS = 1e-5
BIG = -1e30
BUF = 3
FB = D + H
ZC, CC, FC = 0, DI, DI + CONV
WC = FC + FB
GH = 4
GROUPS = Q * H // GH
LO = 32
LOG_TERMS = 6
SOFT_STEPS = LOG_TERMS + 7


def log1p_coefficients():
    w = (1 - np.cos(np.pi * (np.arange(64) + 0.5) / 64)) / 18
    s = np.sqrt(w)
    fit = np.polynomial.Chebyshev.fit(w, 2 * np.arctanh(s) / s, LOG_TERMS - 1, domain=[0, 1 / 9])
    return [float(c) for c in fit.convert(kind=np.polynomial.Polynomial).coef]


def program(nc, x, w_in, conv_w, conv_b, dt_bias, a_log, d_skip, rms_w, w_out, ln_g, ln_b,
            f1t, f2t, f3, f_bias, out):
    steps = x.shape[1] // P
    x_t = x.rearrange("q t d -> t q d")
    out_t = out.rearrange("q t d -> t q d")
    logc = log1p_coefficients()

    with ExitStack() as ctx:
        def sb(name, shape, dt=F32):
            return ctx.enter_context(nc.sbuf_tensor(name, shape, dt))

        def sem(name):
            return ctx.enter_context(nc.semaphore(name))

        def sems(name, n):
            return [sem(f"{name}{i}") for i in range(n)]

        ring0, ring1, e_bank0, e_bank1, xt_bank, bg_bank, yoff_bank, yd_bank = [
            ctx.enter_context(nc.psum_tensor(n, [P, 512], F32))
            for n in ("ring0", "ring1", "e_bank0", "e_bank1", "xt_bank", "bg_bank", "yoff_bank", "yd_bank")]
        e_bank = [e_bank0, e_bank1]

        nw = KD * (DI + CONV + H)
        lay1 = sb("lay1", [P, 2 * Q * H * P])
        lay2 = sb("lay2", [P, 4 * Q * DI])
        win = lay1[:, 0:nw].rearrange("p (k n) -> p k n", k=KD)
        wh = sb("wh", [P, KD, WC], F32R)
        wl = sb("wl", [P, KD, WC], F32R)
        nf = KD * D
        nsel = 2 * H * P
        f1s = lay1[:, nw:nw + nf].rearrange("p (k n) -> p k n", k=KD)
        f2s = lay1[:, nw + nf:nw + 2 * nf].rearrange("p (k n) -> p k n", k=KD)
        sel = lay2[0:LO + 2 * H, 0:nsel].rearrange("p (j t) -> p j t", t=P)
        mask = lay2[:, nsel:nsel + 4 * P].rearrange("p (j t) -> p j t", t=P)
        f3s = lay2[:, nsel + 4 * P:nsel + 4 * P + nf].rearrange("p (k n) -> p k n", k=KD)
        f23 = lay2[:, nsel + 4 * P + nf:nsel + 4 * P + 2 * nf].rearrange("p (k n) -> p k n", k=KD)
        at_g = nsel + 4 * P + 2 * nf
        sel_g = lay2[0:LO + 2 * H, at_g:at_g + GROUPS * P].rearrange("p (g t) -> p g t", t=P)
        brow = sb("brow", [LO + 1, FB])
        bias_r = sb("bias_r", [LO + 1, FB], F32R)
        ones_r = sb("ones_r", [LO + 1, P], F32R)
        wo = sb("wo", [P, KI, D])
        rmsw = sb("rmsw", [P, KI])
        cw = sb("cw", [P, CT, TAPS])
        cb = sb("cb", [P, CT])
        a_neg = sb("a_neg", [P, Q * H])
        d_bc = sb("d_bc", [P, H])
        lng = sb("lng", [P, D])
        lnb = sb("lnb", [P, D])
        ident = sb("ident", [P, P])
        ident_r = sb("ident_r", [P, P], F32R)
        ones = sb("ones", [P, P])
        upto = sb("upto", [P, P])
        after = sb("after", [P, P])
        mask_r = sb("mask_r", [P, 4 * P], F32R)
        sel_r = sb("sel_r", [LO + Q * H, GROUPS, P], F32R)
        own = sb("own", [LO + Q * H, GH])
        nhalf = sb("nhalf", [P, 2])

        xin = sb("xin", [P, BUF, Q, D])
        xn = sb("xn", [P, BUF, Q, D])
        raw = sb("raw", [P, BUF, CT, Q, HALO + P])
        xs = sb("xs", [P, BUF, CT, Q, P])
        gate = sb("gate", [P, BUF, Q, DI])
        res = sb("res", [P, BUF, Q, D])
        dts = sb("dts", [P, BUF, Q * H])
        exs = sb("exs", [P, BUF, 3 * Q * H])
        obuf = sb("obuf", [P, BUF, Q, D])
        xh = sb("xh", [P, KD, Q, P], F32R)
        xl = sb("xl", [P, KD, Q, P], F32R)
        u = sb("u", [P, CT, Q, P])
        ft = sb("ft", [P, Q, D])
        st1 = sb("st1", [P, Q, 6])
        mv1 = sb("mv1", [P, Q, 2])
        ve1 = sb("ve1", [P, Q])
        rs1 = sb("rs1", [P, Q])
        v16 = sb("v16", [P, Q, H])
        nab = sb("nab", [P, Q * H])
        ee = sb("ee", [P, Q * H])
        den = sb("den", [P, Q * H])
        rc = sb("rc", [P, Q * H])
        relu = sb("relu", [P, Q * H])
        sv = sb("sv", [P, Q * H])
        ww = sb("ww", [P, Q * H])
        pa = sb("pa", [P, Q * H])
        pb = sb("pb", [P, Q * H])
        a48 = sb("a48", [P, LO + Q * H])
        w16 = sb("w16", [P, Q * H])
        ncs = sb("ncs", [P, Q * H])
        rows = sb("rows", [LO + Q * H, P], F32R)
        spread = sb("spread", [LO + Q * H, GH, P], F32R)
        xsb = sb("xsb", [P, Q, DI])
        xdt = sb("xdt", [P, Q, DI])
        xw = sb("xw", [P, Q, DI])
        xd = sb("xd", [P, Q, DI])
        btg = sb("btg", [P, Q, 2 * P])
        el, mm = (lay1[:, i * Q * H * P:(i + 1) * Q * H * P].rearrange("p (q h t) -> p q h t", q=Q, h=H)
                  for i in range(2))
        state = sb("state", [P, Q, DI])
        sdec = sb("sdec", [P, Q, DI])
        t1, t2, y, yg = (lay2[:, i * Q * DI:(i + 1) * Q * DI].rearrange("p (q n) -> p q n", q=Q) for i in range(4))
        junk = sb("junk", [P, DI])
        ss = sb("ss", [P, Q])
        sse = sb("sse", [P, Q])
        rr = sb("rr", [P, Q])
        yts = sb("yts", [P, Q, KI, P])
        hh = sb("hh", [P, Q, D])
        st2 = sb("st2", [P, Q, 6])
        mv2 = sb("mv2", [P, Q, 2])
        ve2 = sb("ve2", [P, Q])
        rs2 = sb("rs2", [P, Q])

        s_load = sem("s_load")
        s_gp = sem("s_gp")
        s_const = sem("s_const")
        s_high = sem("s_high")
        s_sel = sem("s_sel")
        s_split = sem("s_split")
        s_f23 = sem("s_f23")
        s_f23s = sem("s_f23s")
        s_f123 = sem("s_f123")
        s_fhigh = sem("s_fhigh")
        s_an = sem("s_an")
        s_apart = sem("s_apart")
        x_loaded = sems("x_loaded", BUF)
        stored = sems("stored", BUF)
        st1_done, mv1_done, ve1_done, rs1_done, xn_done = map(sem, ("st1_done", "mv1_done", "ve1_done", "rs1_done", "xn_done"))
        xt_in_psum, xh_done, xl_done = map(sem, ("xt_in_psum", "xh_done", "xl_done"))
        f_in_psum, f_read, z_in_psum, zt_done, gate_done = (sems(n, Q) for n in ("f_in_psum", "f_read", "z_in_psum", "zt_done", "gate_done"))
        c_in_psum, raw_done, th_done, xs_done = (sems(n, NG) for n in ("c_in_psum", "raw_done", "th_done", "xs_done"))
        tap_done = [sems(f"tap_done{t}_", NG) for t in range(HALO)]
        halo_done, ee_done = map(sem, ("halo_done", "ee_done"))
        soft = sems("soft", SOFT_STEPS - 1)
        a_done, res_chain, res_done = map(sem, ("a_done", "res_chain", "res_done"))
        sums_in_psum, sums_read, rows_done, spread_done, w16_done, total_done = map(
            sem, ("sums_in_psum", "sums_read", "rows_done", "spread_done", "w16_done", "total_done"))
        (xt2_in_psum, xsb_done, xdt_done, xw_done, xd_done, sdec_done, bg_in_psum, bg_read, yoff_in_psum, t1_done,
         t2_done, st_in_psum, state_done, yd_in_psum, y_done, yg_done, ss_done, sse_done, rr_done, yt_in_psum, yts_done,
         o_in_psum, h_done, st2_done, mv2_done, ve2_done, rs2_done, hn_done, hg_done, out_done) = (
            sems(n, Q) for n in (
                "xt2_in_psum", "xsb_done", "xdt_done", "xw_done", "xd_done", "sdec_done", "bg_in_psum", "bg_read",
                "yoff_in_psum", "t1_done", "t2_done", "st_in_psum", "state_done", "yd_in_psum", "y_done", "yg_done",
                "ss_done", "sse_done", "rr_done", "yt_in_psum", "yts_done", "o_in_psum", "h_done", "st2_done",
                "mv2_done", "ve2_done", "rs2_done", "hn_done", "hg_done", "out_done"))
        e_in_psum, e_done, m_done = ([sems(f"{n}{q}_", 2) for q in range(Q)] for n in ("e_in_psum", "e_done", "m_done"))

        def begun(step):
            return not isinstance(step, int) or step >= 0

        def apart(eng):
            eng.sem_inc(s_apart, 1)

        def live(step):
            return not isinstance(step, int) or 0 <= step < steps

        def before(k, q):
            return (k, 0) if q else (k - 1, 1)

        first, last = BUF, (steps - 2) // BUF * BUF

        def passes(eng, one_pass):
            for k in range(-2, first):
                one_pass(k, k % BUF)
            with eng.Fori(first // BUF, last // BUF) as i:
                for b in range(BUF):
                    one_pass(i * BUF + b, b)
            for k in range(last, steps + 2):
                one_pass(k, k % BUF)

        def heads(ap):
            return ap.rearrange("p (h c) -> p h c", h=H)

        def per_head(ap):
            return ap.unsqueeze(2).to_broadcast([P, H, HD])

        def count16(k, b):
            if isinstance(k, int):
                return 16 * (k // BUF + 1)
            return (k - b) // BUF * 16 + 16

        block = ctx.enter_context(nc.Block())

        @block.sync
        def _(sp):
            for b in range(BUF):
                sp.sem_inc(stored[b], 16)

            def load(step, b, rows_at):
                sp.dma_start(xin[:, b], x_t[rows_at, :, :]).then_inc(x_loaded[b], 16)

            for j in range(BUF):
                load(j, j, slice(j * P, (j + 1) * P))
            loads = [
                (win[:, :, :], w_in.rearrange("(k p) n -> p k n", p=P)),
                (f1s[:, :, :], f1t.rearrange("(k p) n -> p k n", p=P)),
                (f2s[:, :, :], f2t.rearrange("(k p) n -> p k n", p=P)),
                (f3s[:, :, :], f3.rearrange("(k p) n -> p k n", p=P)),
                (wo[:, :, :], w_out.rearrange("(k p) n -> p k n", p=P)),
                (rmsw[:, :], rms_w), (cw[:, :, :], conv_w.rearrange("(k p) n -> p k n", p=P)), (cb[:, :], conv_b),
                (a_neg[:, 0:H], a_log.partition_broadcast(P)),
                (a_neg[:, H:2 * H], a_log.partition_broadcast(P)), (d_bc[:, :], d_skip.partition_broadcast(P)),
                (lng[:, :], ln_g.partition_broadcast(P)), (lnb[:, :], ln_b.partition_broadcast(P)),
            ]
            for dst, src in loads:
                sp.dma_start(dst, src).then_inc(s_load, 16)
            sp.wait_ge(s_gp, 1)
            for row in (0, LO):
                sp.dma_start(brow[row:row + 1, 0:D], f_bias.rearrange("(a n) -> a n", a=1)).then_inc(s_load, 16)
                sp.dma_start(brow[row:row + 1, D:FB], dt_bias.rearrange("(a n) -> a n", a=1)).then_inc(s_load, 16)

            def rows_of(step):
                return slice(step * P, (step + 1) * P) if isinstance(step, int) else bass.ds(step * P, P)

            def one_pass(k, b, loads_on=True):
                b1 = (b + 1) % BUF
                if live(k + 1) and loads_on and live(k + 1 + BUF):
                    sp.wait_ge(res_done, k + 2)
                    load(k + 1 + BUF, b1, rows_of(k + 1 + BUF))
                if live(k - 1):
                    sp.wait_ge(out_done[0], k)
                    sp.wait_ge(out_done[1], k)
                    bo = (b - 1) % BUF
                    sp.dma_start(out_t[rows_of(k - 1), :, :], obuf[:, bo]).then_inc(stored[bo], 16)

            stop = (steps - 1 - BUF) // BUF * BUF
            for k in range(-2, first):
                one_pass(k, k % BUF)
            with sp.Fori(first // BUF, stop // BUF) as i:
                for b in range(BUF):
                    one_pass(i * BUF + b, b)
            for k in range(stop, steps + 1):
                one_pass(k, k % BUF)
            for b in range(BUF):
                sp.wait_ge(stored[b], 16 + 16 * len(range(b, steps, BUF)))

        n_loads = 13 + 4

        @block.gpsimd
        def _(pool):
            g = nc.gpsimd
            g.memset(brow[:, :], 0.0).then_inc(s_gp, 1)
            g.memset(ident[:, :], 0.0).then_inc(s_gp, 1)
            g.memset(ones[:, :], 1.0).then_inc(s_gp, 1)
            g.memset(mask[:, :, :], 0.0).then_inc(s_gp, 1)
            g.memset(sel[:, :, :], 0.0).then_inc(s_gp, 1)
            g.memset(nhalf[:, :], -0.5).then_inc(s_gp, 1)
            g.memset(a48[:, :], 0.0).then_inc(s_gp, 1)
            g.memset(state[:, :, :], 0.0).then_inc(s_gp, 1)
            g.memset(raw[:, 0, :, :, 0:HALO], 0.0).then_inc(halo_done, 1)
            pool.wait_ge(s_gp, 8)
            g.affine_select(out=ident[:, :], in_=ident[:, :], compare_op=ALU.not_equal, fill=1.0, base=0,
                            pattern=[[-1, P]], channel_multiplier=1).then_inc(s_gp, 1)
            g.affine_select(out=upto[:, :], in_=ones[:, :], compare_op=ALU.is_ge, fill=0.0, base=0,
                            pattern=[[1, P]], channel_multiplier=-1).then_inc(s_gp, 1)
            g.affine_select(out=after[:, :], in_=ones[:, :], compare_op=ALU.is_gt, fill=0.0, base=0,
                            pattern=[[-1, P]], channel_multiplier=1).then_inc(s_gp, 1)
            g.affine_select(out=mask[:, :, :], in_=mask[:, :, :], compare_op=ALU.is_ge, fill=BIG, base=0,
                            pattern=[[0, 4], [1, P]], channel_multiplier=-1).then_inc(s_gp, 1)
            g.affine_select(out=sel[:, :, :], in_=sel[:, :, :], compare_op=ALU.not_equal, fill=1.0, base=0,
                            pattern=[[-1, Q * H], [0, P]], channel_multiplier=1).then_inc(s_gp, 1)
            pool.wait_ge(s_gp, 13)
            g.affine_select(out=sel[:, :, :], in_=sel[:, :, :], compare_op=ALU.not_equal, fill=1.0, base=-LO,
                            pattern=[[-1, Q * H], [0, P]], channel_multiplier=1).then_inc(s_const, 1)
            pool.wait_ge(s_load, 16 * n_loads)
            pool.wait_ge(s_split, 1)

            def layer_norm_scale(k):
                pool.wait_ge(mv1_done, k + 1)
                apart(pool)
                g.tensor_scalar(ve1[:, :], mv1[:, :, 1], EPS, 1.0, ALU.add, ALU.mult).then_inc(ve1_done, 1)
                pool.wait_ge(ve1_done, k + 1)
                g.tensor_tensor(rs1[:, :], ve1[:, :], nhalf[:, :], ALU.pow).then_inc(rs1_done, 1)

            def halo(k, b):
                for c in range(NG):
                    if begun(k - 1):
                        pool.wait_ge(raw_done[c], k)
                pb_ = (b - 1) % BUF
                if not isinstance(k, int) or k > 0:
                    apart(pool)
                    g.tensor_copy(raw[:, b, :, :, 0:HALO], raw[:, pb_, :, :, P:P + HALO]).then_inc(halo_done, 1)

            def residual(k, b):
                pool.wait_ge(f_read[0], k + 1)
                pool.wait_ge(f_read[1], k + 1)
                if begun(k - BUF):
                    pool.wait_ge(out_done[0], k - BUF + 1)
                    pool.wait_ge(out_done[1], k - BUF + 1)
                g.tensor_tensor(res[:, b], xin[:, b], ft[:, :, :], ALU.add).then_inc(res_chain, 1)

            def residual_bias(k, b):
                pool.wait_ge(res_chain, k + 1)
                g.tensor_tensor(res[:, b], res[:, b], lnb[:, :].unsqueeze(1).to_broadcast([P, Q, D]), ALU.add)\
                    .then_inc(res_done, 1)

            def state_weights(k, b):
                pool.wait_ge(sums_read, k + 1)
                if begun(k - 1):
                    pool.wait_ge(xw_done[0], k)
                    pool.wait_ge(xw_done[1], k)
                g.tensor_tensor(w16[:, :], dts[:, b], exs[:, b, Q * H:2 * Q * H], ALU.mult).then_inc(w16_done, 1)
                g.tensor_tensor(exs[:, b, 2 * Q * H:3 * Q * H], exs[:, b, 0:Q * H], exs[:, b, Q * H:2 * Q * H], ALU.mult)\
                    .then_inc(total_done, 1)

            def spread_rows(k):
                pool.wait_ge(rows_done, k + 1)
                if begun(k - 1):
                    pool.wait_ge(e_in_psum[1][0], k)
                    pool.wait_ge(e_in_psum[1][1], k)
                shape = [LO + Q * H, GH, P]
                g.tensor_tensor(spread[:, :, :], rows[:, :].bitcast(F32).unsqueeze(1).to_broadcast(shape),
                                own[:, :].unsqueeze(2).to_broadcast(shape), ALU.mult).then_inc(spread_done, 1)

            def scale_x(k, q):
                pool.wait_ge(xsb_done[q], k + 1)
                if q == 0:
                    pool.wait_ge(w16_done, k + 1)
                g.tensor_tensor(heads(xw[:, q]), heads(xsb[:, q]), per_head(w16[:, q * H:(q + 1) * H]), ALU.mult)\
                    .then_inc(xw_done[q], 1)

            def x_times_dt(k, b, q):
                pool.wait_ge(xsb_done[q], k + 1)
                if begun(k - 1):
                    pool.wait_ge(yd_in_psum[q], k)
                g.tensor_tensor(heads(xdt[:, q]), heads(xsb[:, q]), per_head(dts[:, b, q * H:(q + 1) * H]), ALU.mult)\
                    .then_inc(xdt_done[q], 1)

            def decay_state(k, b, q):
                if begun(k - 1):
                    pool.wait_ge(state_done[q], k)
                pool.wait_ge(total_done, k + 1)
                g.tensor_tensor(heads(sdec[:, q]), heads(state[:, q]),
                                per_head(exs[:, b, 2 * Q * H + q * H:2 * Q * H + (q + 1) * H]), ALU.mult)\
                    .then_inc(sdec_done[q], 1)

            def skip_x(k, q):
                pool.wait_ge(xsb_done[q], k + 1)
                if begun(k - 1):
                    pool.wait_ge(t2_done[q], k)
                g.tensor_tensor(heads(xd[:, q]), heads(xsb[:, q]), per_head(d_bc[:, :]), ALU.mult)\
                    .then_inc(xd_done[q], 1)

            def add_skip(k, q):
                pool.wait_ge(t1_done[q], k + 1)
                pool.wait_ge(xd_done[q], k + 1)
                g.tensor_tensor(t2[:, q], t1[:, q], xd[:, q], ALU.add).then_inc(t2_done[q], 1)

            def rms_scale(k, q):
                pool.wait_ge(ss_done[q], k + 1)
                apart(pool)
                g.tensor_scalar(sse[:, q:q + 1], ss[:, q:q + 1], 1.0 / DI, EPS, ALU.mult, ALU.add).then_inc(sse_done[q], 1)
                pool.wait_ge(sse_done[q], k + 1)
                g.tensor_tensor(rr[:, q:q + 1], sse[:, q:q + 1], nhalf[:, 0:1], ALU.pow).then_inc(rr_done[q], 1)

            def last_norm_scale(k, q):
                pool.wait_ge(mv2_done[q], k + 1)
                apart(pool)
                g.tensor_scalar(ve2[:, q:q + 1], mv2[:, q, 1:2], EPS, 1.0, ALU.add, ALU.mult).then_inc(ve2_done[q], 1)
                pool.wait_ge(ve2_done[q], k + 1)
                g.tensor_tensor(rs2[:, q:q + 1], ve2[:, q:q + 1], nhalf[:, 0:1], ALU.pow).then_inc(rs2_done[q], 1)

            def output(k, b, q):
                pool.wait_ge(hn_done[q], k + 1)
                if q == 0:
                    pool.wait_ge(stored[b], count16(k, b))
                g.tensor_tensor(obuf[:, b, q], hh[:, q], lng[:, :], ALU.mult).then_inc(hg_done[q], 1)
                pool.wait_ge(hg_done[q], k + 1)
                g.tensor_tensor(obuf[:, b, q], obuf[:, b, q], res[:, b, q], ALU.add).then_inc(out_done[q], 1)

            def one_pass(k, b):
                b1, bo = (b + 1) % BUF, (b - 1) % BUF
                if live(k - 2):
                    last_norm_scale(k - 2, 0)
                if live(k - 1):
                    skip_x(k - 1, 1)
                    decay_state(k - 1, bo, 1)
                if live(k - 2):
                    last_norm_scale(k - 2, 1)
                    output(k - 2, b1, 0)
                if live(k + 2):
                    layer_norm_scale(k + 2)
                if live(k):
                    spread_rows(k)
                if live(k - 1):
                    scale_x(k - 1, 1)
                    add_skip(k - 1, 1)
                if live(k + 1):
                    halo(k + 1, b1)
                if live(k - 1):
                    rms_scale(k - 1, 0)
                if live(k - 2):
                    output(k - 2, b1, 1)
                if live(k):
                    skip_x(k, 0)
                    x_times_dt(k, b, 0)
                if live(k + 1):
                    residual(k + 1, b1)
                if live(k):
                    state_weights(k, b)
                    residual_bias(k, b)
                    add_skip(k, 0)
                if live(k - 1):
                    rms_scale(k - 1, 1)
                if live(k):
                    decay_state(k, b, 0)
                    x_times_dt(k, b, 1)
                    scale_x(k, 0)

            passes(pool, one_pass)

        @block.vector
        def _(dve):
            v = nc.vector
            dve.wait_ge(s_load, 16 * n_loads)
            dve.wait_ge(s_an, 1)
            v.tensor_scalar(a_neg[:, :], a_neg[:, :], -1.0, None, ALU.mult).then_inc(s_split, 1)
            parts = [(win[:, :, 0:DI], ZC, DI, 0.5), (win[:, :, DI:DI + CONV], CC, CONV, 1.0),
                     (win[:, :, DI + CONV:DI + CONV + H], FC + D, H, 1.0)]
            for src, at, n, scale in (parts[0], parts[2]):
                v.tensor_scalar(wh[:, :, at:at + n], src, scale, None, ALU.mult).then_inc(s_high, 1)
            v.tensor_copy(bias_r[:, :], brow[:, :]).then_inc(s_high, 1)
            dve.wait_ge(s_const, 1)
            v.tensor_copy(ident_r[:, :], ident[:, :])
            v.tensor_copy(mask_r[:, :], mask[:, :, :].rearrange("p a t -> p (a t)"))
            v.tensor_reduce(sel_g[:, :, :], sel[:, :, :].rearrange("p (g j) t -> p g t j", j=GH), AXIS.X, ALU.add)
            v.tensor_reduce(own[:, :], sel[:, :, 0].rearrange("p (g j) -> p j g", j=GH), AXIS.X, ALU.add).then_inc(s_sel, 1)
            v.tensor_copy(ones_r[:, :], ones[0:LO + 1, :])
            dve.wait_ge(s_high, 4)
            dve.wait_ge(s_sel, 1)
            v.tensor_copy(sel_r[:, :, :], sel_g[:, :, :])
            for src, at, n, scale in parts:
                for kd in range(KD):
                    v.scalar_tensor_tensor(out=wl[:, kd, at:at + n], in0=src[:, kd], scalar=scale,
                                           in1=wh[:, kd, at:at + n].bitcast(F32), op0=ALU.mult, op1=ALU.subtract)
            v.tensor_tensor(bias_r[LO:LO + 1, :], brow[LO:LO + 1, :], bias_r[LO:LO + 1, :].bitcast(F32), ALU.subtract)
            for ki in range(KI):
                v.tensor_scalar(wo[:, ki], wo[:, ki], rmsw[:, ki:ki + 1], None, ALU.mult)
            v.tensor_scalar(cw[:, :, :], cw[:, :, :], 0.5, None, ALU.mult)
            v.tensor_scalar(cb[:, :], cb[:, :], 0.5, None, ALU.mult)
            for m, bank in enumerate((ring0, ring1)):
                dve.wait_ge(s_fhigh, m + 1)
                last = v.tensor_tensor(wl[:, m, FC:FC + D], bank[:, 0:D], wh[:, m, FC:FC + D].bitcast(F32), ALU.subtract)
            last.then_inc(s_split, 1)
            dve.wait_ge(s_split, 2)

            def norm_stats(k, b):
                dve.wait_ge(x_loaded[b], count16(k, b))
                for q in range(Q):
                    last = v.bn_stats(st1[:, q], xin[:, b, q])
                last.then_inc(st1_done, 1)

            def norm_mean_var(k):
                dve.wait_ge(st1_done, k + 1)
                apart(dve)
                for q in range(Q):
                    last = v.bn_aggr(mv1[:, q], st1[:, q])
                last.then_inc(mv1_done, 1)

            def norm_apply(k, b):
                if begun(k - BUF):
                    dve.wait_ge(h_done[1], k - BUF + 1)
                dve.wait_ge(rs1_done, k + 1)
                for q in range(Q):
                    last = v.tensor_scalar(xn[:, b, q], xin[:, b, q], mv1[:, q, 0:1], rs1[:, q:q + 1],
                                           ALU.subtract, ALU.mult)
                last.then_inc(xn_done, 1)

            def low_part(k):
                dve.wait_ge(xh_done, k + 1)
                v.tensor_tensor(xl[:, :, :, :].rearrange("p k q t -> p (k q t)"), ring1[:, :],
                                xh[:, :, :, :].rearrange("p k q t -> p (k q t)").bitcast(F32), ALU.subtract)\
                    .then_inc(xl_done, 1)

            def tap(k, b, c, t):
                if t == 0:
                    dve.wait_ge(raw_done[c], k + 1)
                    dve.wait_ge(halo_done, k + 1)
                else:
                    dve.wait_ge(tap_done[t - 1][c], k + 1)
                for ct in (2 * c, 2 * c + 1):
                    last = v.scalar_tensor_tensor(out=u[:, ct], in0=raw[:, b, ct, :, t:t + P], scalar=cw[:, ct, t:t + 1],
                                                  in1=u[:, ct], op0=ALU.mult, op1=ALU.add)
                last.then_inc(tap_done[t][c], 1)

            def silu(k, b, c):
                dve.wait_ge(th_done[c], k + 1)
                part = slice(2 * c, 2 * c + 2)
                v.scalar_tensor_tensor(out=xs[:, b, part].rearrange("p c q t -> p (c q t)"),
                                       in0=xs[:, b, part].rearrange("p c q t -> p (c q t)"), scalar=1.0,
                                       in1=u[:, part].rearrange("p c q t -> p (c q t)"),
                                       op0=ALU.add, op1=ALU.mult).then_inc(xs_done[c], 1)

            def gates(k, b, q):
                dve.wait_ge(zt_done[q], k + 1)
                bank = (ring1, ring0)[q]
                v.scalar_tensor_tensor(out=gate[:, b, q], in0=gate[:, b, q], scalar=1.0, in1=bank[:, :],
                                       op0=ALU.add, op1=ALU.mult).then_inc(gate_done[q], 1)

            def softplus(k, b, i):
                vec = v16[:, :, :].rearrange("p q h -> p (q h)")
                if i == 0:
                    dve.wait_ge(f_read[0], k + 1)
                    dve.wait_ge(f_read[1], k + 1)
                    v.tensor_scalar(relu[:, :], vec, 0.0, None, ALU.max)
                    ins = v.scalar_tensor_tensor(out=nab[:, :], in0=vec, scalar=-1.0, in1=vec, op0=ALU.mult, op1=ALU.min)
                elif i == 1:
                    dve.wait_ge(ee_done, k + 1)
                    ins = v.tensor_scalar(den[:, :], ee[:, :], 2.0, None, ALU.add)
                else:
                    dve.wait_ge(soft[i - 1], k + 1)
                    if i == 2:
                        ins = v.reciprocal(rc[:, :], den[:, :])
                    elif i == 3:
                        ins = v.tensor_tensor(sv[:, :], ee[:, :], rc[:, :], ALU.mult)
                    elif i == 4:
                        ins = v.tensor_tensor(ww[:, :], sv[:, :], sv[:, :], ALU.mult)
                    elif i == 5:
                        ins = v.tensor_scalar(pa[:, :], ww[:, :], logc[-1], None, ALU.mult)
                    elif i < 4 + LOG_TERMS:
                        ins = v.scalar_tensor_tensor(out=pa[:, :], in0=pa[:, :], scalar=logc[4 - i], in1=ww[:, :],
                                                     op0=ALU.add, op1=ALU.mult)
                    elif i == 4 + LOG_TERMS:
                        ins = v.scalar_tensor_tensor(out=pb[:, :], in0=pa[:, :], scalar=logc[0], in1=sv[:, :],
                                                     op0=ALU.add, op1=ALU.mult)
                    elif i == 5 + LOG_TERMS:
                        ins = v.tensor_tensor(dts[:, b], pb[:, :], relu[:, :], ALU.add)
                    else:
                        for at in (0, LO):
                            ins = v.tensor_tensor(a48[:, at:at + Q * H], dts[:, b], a_neg[:, :], ALU.mult)
                        ins.then_inc(a_done, 1)
                        return
                ins.then_inc(soft[i], 1)

            def low_rows(k):
                dve.wait_ge(sums_read, k + 1)
                v.tensor_tensor(rows[LO:LO + Q * H, :], bg_bank[LO:LO + Q * H, 64:64 + P],
                                rows[LO:LO + Q * H, :].bitcast(F32), ALU.subtract).then_inc(rows_done, 1)

            def weigh(k, q, half):
                dve.wait_ge(e_done[q][half], k + 1)
                dve.wait_ge(bg_read[q], k + 1)
                hs = slice(4 * half, 4 * half + 4)
                v.tensor_tensor(mm[:, q, hs], el[:, q, hs], btg[:, q, P:2 * P].unsqueeze(1).to_broadcast([P, 4, P]),
                                ALU.mult).then_inc(m_done[q][half], 1)

            def scale_off(k, b, q):
                dve.wait_ge(yoff_in_psum[q], k + 1)
                v.tensor_tensor(heads(t1[:, q]), heads(yoff_bank[:, :]), per_head(exs[:, b, q * H:(q + 1) * H]), ALU.mult)\
                    .then_inc(t1_done[q], 1)

            def new_state(k, q):
                dve.wait_ge(st_in_psum[q], k + 1)
                dve.wait_ge(sdec_done[q], k + 1)
                v.tensor_tensor(state[:, q], xt_bank[:, :], sdec[:, q], ALU.add).then_inc(state_done[q], 1)

            def add_diag(k, q):
                dve.wait_ge(yd_in_psum[q], k + 1)
                dve.wait_ge(t2_done[q], k + 1)
                v.tensor_tensor(y[:, q], yd_bank[:, :], t2[:, q], ALU.add).then_inc(y_done[q], 1)

            def apply_gate(k, b, q):
                dve.wait_ge(y_done[q], k + 1)
                v.tensor_tensor(yg[:, q], y[:, q], gate[:, b, q], ALU.mult).then_inc(yg_done[q], 1)

            def last_h(k, b, q):
                if begun(k - 1):
                    dve.wait_ge(hg_done[q], k)
                dve.wait_ge(o_in_psum[q], k + 1)
                dve.wait_ge(rr_done[q], k + 1)
                v.scalar_tensor_tensor(out=hh[:, q], in0=yoff_bank[:, 0:D], scalar=rr[:, q:q + 1], in1=xn[:, b, q],
                                       op0=ALU.mult, op1=ALU.add).then_inc(h_done[q], 1)

            def last_stats(k, q):
                dve.wait_ge(h_done[q], k + 1)
                v.bn_stats(st2[:, q], hh[:, q]).then_inc(st2_done[q], 1)

            def last_mean_var(k, q):
                dve.wait_ge(st2_done[q], k + 1)
                apart(dve)
                v.bn_aggr(mv2[:, q], st2[:, q]).then_inc(mv2_done[q], 1)

            def last_apply(k, q):
                dve.wait_ge(rs2_done[q], k + 1)
                v.tensor_scalar(hh[:, q], hh[:, q], mv2[:, q, 0:1], rs2[:, q:q + 1], ALU.subtract, ALU.mult)\
                    .then_inc(hn_done[q], 1)

            def one_pass(k, b):
                b1, b2, bo = (b + 1) % BUF, (b + 2) % BUF, (b - 1) % BUF
                if live(k - 1):
                    weigh(k - 1, 1, 1)
                if live(k - 2):
                    last_apply(k - 2, 0)
                if live(k + 2):
                    norm_stats(k + 2, b2)
                if live(k):
                    silu(k, b, 0)
                if live(k + 2):
                    norm_mean_var(k + 2)
                if live(k):
                    tap(k, b, 2, 2)
                if live(k - 2):
                    last_apply(k - 2, 1)
                if live(k + 1):
                    softplus(k + 1, b1, 0)
                if live(k):
                    low_rows(k)
                if live(k - 1):
                    weigh(k - 1, 1, 0)
                    scale_off(k - 1, bo, 1)
                if live(k):
                    silu(k, b, 2)
                if live(k + 1):
                    softplus(k + 1, b1, 1)
                if live(k - 1):
                    new_state(k - 1, 0)
                if live(k):
                    silu(k, b, 1)
                if live(k + 1):
                    softplus(k + 1, b1, 2)
                    softplus(k + 1, b1, 3)
                if live(k - 1):
                    add_diag(k - 1, 1)
                if live(k + 1):
                    tap(k + 1, b1, 0, 0)
                if live(k - 1):
                    apply_gate(k - 1, bo, 1)
                if live(k + 1):
                    softplus(k + 1, b1, 4)
                if live(k - 1):
                    last_h(k - 1, bo, 0)
                if live(k + 1):
                    softplus(k + 1, b1, 5)
                    tap(k + 1, b1, 0, 1)
                    tap(k + 1, b1, 1, 0)
                    tap(k + 1, b1, 0, 2)
                if live(k - 1):
                    last_stats(k - 1, 0)
                if live(k + 1):
                    softplus(k + 1, b1, 6)
                if live(k - 1):
                    new_state(k - 1, 1)
                if live(k + 1):
                    softplus(k + 1, b1, 7)
                if live(k):
                    scale_off(k, b, 0)
                if live(k + 1):
                    tap(k + 1, b1, 1, 1)
                    softplus(k + 1, b1, 8)
                if live(k):
                    weigh(k, 0, 0)
                if live(k + 1):
                    softplus(k + 1, b1, 9)
                    tap(k + 1, b1, 1, 2)
                    gates(k + 1, b1, 0)
                if live(k):
                    weigh(k, 0, 1)
                if live(k - 1):
                    last_h(k - 1, bo, 1)
                if live(k + 2):
                    norm_apply(k + 2, b2)
                if live(k - 1):
                    last_stats(k - 1, 1)
                if live(k + 1):
                    softplus(k + 1, b1, 10)
                    tap(k + 1, b1, 2, 0)
                if live(k - 1):
                    last_mean_var(k - 1, 0)
                if live(k + 1):
                    softplus(k + 1, b1, 11)
                    tap(k + 1, b1, 2, 1)
                if live(k + 2):
                    low_part(k + 2)
                if live(k - 1):
                    last_mean_var(k - 1, 1)
                if live(k):
                    add_diag(k, 0)
                if live(k + 1):
                    softplus(k + 1, b1, SOFT_STEPS - 1)
                if live(k):
                    apply_gate(k, b, 0)
                if live(k + 1):
                    gates(k + 1, b1, 1)

            passes(dve, one_pass)

        @block.scalar
        def _(act):
            s = nc.scalar
            act.wait_ge(s_load, 16 * n_loads)
            s.activation(a_neg[:, :], a_neg[:, :], ACT.Exp).then_inc(s_an, 1)
            s.activation(wh[:, :, CC:CC + CONV], win[:, :, DI:DI + CONV], ACT.Copy).then_inc(s_high, 1)
            for m, bank in enumerate((ring0, ring1)):
                act.wait_ge(s_f23, m + 1)
                s.activation(f23[:, m, :], bank[:, 0:D], ACT.Copy).then_inc(s_f23s, 1)
            for m, bank in enumerate((ring0, ring1)):
                act.wait_ge(s_f123, m + 1)
                s.activation(wh[:, m, FC:FC + D], bank[:, 0:D], ACT.Copy).then_inc(s_fhigh, 1)
            act.wait_ge(s_split, 2)

            def high_part(k):
                act.wait_ge(xt_in_psum, k + 1)
                s.activation(xh[:, :, :, :].rearrange("p k q t -> p (k q t)"), ring1[:, :], ACT.Copy).then_inc(xh_done, 1)

            def branch(k, q):
                act.wait_ge(f_in_psum[q], k + 1)
                bank = (ring0, ring1)[q]
                if begun(k - 1):
                    act.wait_ge(res_chain, k)
                s.activation(ft[:, q], bank[:, 0:D], ACT.Tanh)
                s.activation(v16[:, q], bank[:, D:FB], ACT.Copy).then_inc(f_read[q], 1)

            def conv_in(k, b, c):
                act.wait_ge(c_in_psum[c], k + 1)
                bank = (ring0, ring1, ring0)[c]
                if begun(k - 1):
                    act.wait_ge(xs_done[c], k)
                for i, ct in enumerate((2 * c, 2 * c + 1)):
                    s.activation(u[:, ct].rearrange("p q t -> p (q t)"), bank[:, i * Q * P:(i + 1) * Q * P], ACT.Identity,
                                 bias=cb[:, ct:ct + 1], scale=cw[:, ct, HALO:TAPS])
                s.activation(raw[:, b, 2 * c:2 * c + 2, :, HALO:], bank[:, :].rearrange("p (c q t) -> p c q t", c=2, q=Q),
                             ACT.Copy).then_inc(raw_done[c], 1)

            def softplus_exp(k):
                act.wait_ge(soft[0], k + 1)
                s.activation(ee[:, :], nab[:, :], ACT.Exp).then_inc(ee_done, 1)

            def conv_tanh(k, b, c):
                act.wait_ge(tap_done[HALO - 1][c], k + 1)
                part = slice(2 * c, 2 * c + 2)
                s.activation(xs[:, b, part], u[:, part], ACT.Tanh).then_inc(th_done[c], 1)

            def z_tanh(k, b, q):
                act.wait_ge(z_in_psum[q], k + 1)
                bank = (ring1, ring0)[q]
                s.activation(gate[:, b, q], bank[:, :], ACT.Tanh).then_inc(zt_done[q], 1)

            def sums(k, b):
                act.wait_ge(sums_in_psum, k + 1)
                if begun(k - 1):
                    act.wait_ge(e_done[1][0], k)
                    act.wait_ge(e_done[1][1], k)
                    act.wait_ge(spread_done, k)
                s.activation(exs[:, b, 0:2 * Q * H], bg_bank[:, 0:2 * Q * H], ACT.Exp)
                s.mul(ncs[:, :], bg_bank[:, 0:Q * H], -1.0)
                s.activation(rows[:, :], bg_bank[0:LO + Q * H, 64:64 + P], ACT.Copy).then_inc(sums_read, 1)

            def x_tokens(k, q):
                act.wait_ge(xt2_in_psum[q], k + 1)
                s.activation(xsb[:, q], xt_bank[:, :], ACT.Copy).then_inc(xsb_done[q], 1)

            def b_and_g(k, q):
                if begun(k - 1):
                    act.wait_ge(st_in_psum[q], k)
                act.wait_ge(bg_in_psum[q], k + 1)
                s.activation(btg[:, q], bg_bank[:, 0:2 * P], ACT.Copy).then_inc(bg_read[q], 1)

            def decay(k, q, half):
                act.wait_ge(e_in_psum[q][half], k + 1)
                if begun(k - 1):
                    act.wait_ge(m_done[q][half], k)
                if q == 0:
                    act.wait_ge(sums_read, k + 1)
                for j in range(4):
                    h = 4 * half + j
                    last = s.activation(el[:, q, h], e_bank[half][:, j * P:(j + 1) * P], ACT.Exp,
                                        bias=ncs[:, q * H + h:q * H + h + 1])
                last.then_inc(e_done[q][half], 1)

            def square(k, q):
                act.wait_ge(yg_done[q], k + 1)
                s.activation(junk[:, :], yg[:, q], ACT.Square, accum_out=ss[:, q:q + 1]).then_inc(ss_done[q], 1)

            def y_channels(k, q):
                act.wait_ge(yt_in_psum[q], k + 1)
                s.activation(yts[:, q].rearrange("p k t -> p (k t)"), yd_bank[:, :], ACT.Copy).then_inc(yts_done[q], 1)

            def one_pass(k, b):
                b1 = (b + 1) % BUF
                if live(k + 1):
                    branch(k + 1, 1)
                if live(k):
                    sums(k, b)
                if live(k + 1):
                    branch(k + 1, 0)
                if live(k):
                    conv_tanh(k, b, 2)
                if live(k - 1):
                    y_channels(k - 1, 0)
                if live(k + 1):
                    softplus_exp(k + 1)
                    conv_in(k + 1, b1, 0)
                if live(k):
                    b_and_g(k, 0)
                if live(k + 1):
                    conv_in(k + 1, b1, 1)
                if live(k):
                    x_tokens(k, 0)
                    decay(k, 0, 1)
                    decay(k, 0, 0)
                if live(k + 1):
                    z_tanh(k + 1, b1, 0)
                if live(k - 1):
                    y_channels(k - 1, 1)
                    square(k - 1, 1)
                if live(k + 1):
                    conv_in(k + 1, b1, 2)
                if live(k):
                    b_and_g(k, 1)
                    x_tokens(k, 1)
                    decay(k, 1, 1)
                if live(k + 2):
                    high_part(k + 2)
                if live(k + 1):
                    z_tanh(k + 1, b1, 1)
                if live(k):
                    decay(k, 1, 0)
                    square(k, 0)
                if live(k + 1):
                    conv_tanh(k + 1, b1, 1)
                    conv_tanh(k + 1, b1, 0)

            passes(act, one_pass)

        @block.tensor
        def _(pe):
            mul, tr = nc.tensor.matmul, nc.tensor.transpose
            pe.wait_ge(s_load, 16 * n_loads)
            for m, bank in enumerate((ring0, ring1)):
                for kd in range(KD):
                    last = mul(bank[:, 0:D], f2s[:, kd, m * P:(m + 1) * P], f3s[:, kd], start=kd == 0, stop=kd == KD - 1)
                last.then_inc(s_f23, 1)
            pe.wait_ge(s_f23s, KD)
            for m, bank in enumerate((ring0, ring1)):
                for kd in range(KD):
                    last = mul(bank[:, 0:D], f1s[:, kd, m * P:(m + 1) * P], f23[:, kd], start=kd == 0, stop=kd == KD - 1)
                last.then_inc(s_f123, 1)
            pe.wait_ge(s_split, 2)

            def transpose_x(k, b):
                pe.wait_ge(xn_done, k + 1)
                if begun(k - 1):
                    pe.wait_ge(gate_done[0], k)
                for kd in range(KD):
                    for q in range(Q):
                        at = (kd * Q + q) * P
                        last = tr(ring1[:, at:at + P], xn[:, b, q, kd * P:(kd + 1) * P], ident[:, :])
                last.then_inc(xt_in_psum, 1)

            def split_products(out, pairs, first=True):
                n = len(pairs)
                for i, (a, c) in enumerate(pairs):
                    last = mul(out, a, c, start=first and i == 0, stop=i == n - 1)
                return last

            def conv_project(k, c):
                if c == 0:
                    pe.wait_ge(f_read[0], k + 1)
                elif c == 1:
                    pe.wait_ge(f_read[1], k + 1)
                else:
                    pe.wait_ge(raw_done[0], k + 1)
                bank = (ring0, ring1, ring0)[c]
                for i, ct in enumerate((2 * c, 2 * c + 1)):
                    cols = slice(CC + ct * P, CC + (ct + 1) * P)
                    pairs = []
                    for kd in range(KD):
                        xh_, xl_ = (t[:, kd].rearrange("p q t -> p (q t)") for t in (xh, xl))
                        pairs += [(wh[:, kd, cols], xh_), (wh[:, kd, cols], xl_), (wl[:, kd, cols], xh_)]
                    last = split_products(bank[:, i * Q * P:(i + 1) * Q * P], pairs)
                last.then_inc(c_in_psum[c], 1)

            def z_project(k, q):
                pe.wait_ge(raw_done[1 + q], k + 1)
                cols = slice(ZC, ZC + DI)
                pairs = []
                for kd in range(KD):
                    pairs += [(xh[:, kd, q], wh[:, kd, cols]), (xh[:, kd, q], wl[:, kd, cols]), (xl[:, kd, q], wh[:, kd, cols])]
                split_products((ring1, ring0)[q][:, :], pairs).then_inc(z_in_psum[q], 1)

            def branch_project(k, q):
                pe.wait_ge(xl_done, k + 1)
                if q == 0:
                    if begun(k - 1):
                        pe.wait_ge(gate_done[1], k)
                bank = (ring0, ring1)[q][:, 0:FB]
                mul(bank, ones_r[:, :], bias_r[:, :], start=True, stop=False)
                cols = slice(FC, FC + FB)
                pairs = []
                for kd in range(KD):
                    pairs += [(xh[:, kd, q], wh[:, kd, cols]), (xh[:, kd, q], wl[:, kd, cols]), (xl[:, kd, q], wh[:, kd, cols])]
                split_products(bank, pairs, first=False).then_inc(f_in_psum[q], 1)

            def sums(k):
                pe.wait_ge(a_done, k + 1)
                if begun(k - 1):
                    pe.wait_ge(bg_read[1], k)
                n = Q * H
                mul(bg_bank[:, 0:n], upto[:, :], a48[:, 0:n], start=True, stop=True)
                mul(bg_bank[:, n:2 * n], after[:, :], a48[:, 0:n], start=True, stop=True)
                mul(bg_bank[0:LO + n, 64:64 + P], a48[:, :], upto[:, :], start=True, stop=True).then_inc(sums_in_psum, 1)

            def x_tokens(k, b, q):
                pe.wait_ge(xs_done[0], k + 1)
                pe.wait_ge(xs_done[1], k + 1)
                if begun(k - 1):
                    pe.wait_ge(state_done[q], k)
                elif q == 1:
                    pe.wait_ge(xsb_done[0], k + 1)
                for ct in range(KI):
                    last = tr(xt_bank[:, ct * P:(ct + 1) * P], xs[:, b, ct, q], ident[:, :])
                last.then_inc(xt2_in_psum[q], 1)

            def b_and_g(k, b, q):
                if q == 0:
                    pe.wait_ge(rows_done, k + 1)
                else:
                    pe.wait_ge(bg_read[0], k + 1)
                pe.wait_ge(xs_done[2], k + 1)
                tr(bg_bank[:, 0:P], xs[:, b, KI, q], ident[:, :])
                mul(bg_bank[:, P:2 * P], xs[:, b, KI, q], xs[:, b, KI + 1, q], start=True, stop=True)\
                    .then_inc(bg_in_psum[q], 1)

            def exponents(k, q, half):
                if q == 0:
                    pe.wait_ge(spread_done, k + 1)
                if begun(k - 1 + q):
                    pe.wait_ge(e_done[1 - q][half], k + q)
                bank = e_bank[half]
                mul(bank[:, :], ident_r[:, :], mask_r[:, :], start=True, stop=False)
                mul(bank[:, :], sel_r[:, 2 * q + half], spread[:, :, :].rearrange("p j t -> p (j t)"), start=False, stop=True)\
                    .then_inc(e_in_psum[q][half], 1)

            def y_off(k, b, q):
                kp, qp = before(*before(k, q))
                if begun(kp):
                    pe.wait_ge(h_done[qp], kp + 1)
                if begun(k - 1):
                    pe.wait_ge(state_done[q], k)
                pe.wait_ge(xs_done[2], k + 1)
                mul(yoff_bank[:, :], xs[:, b, KI + 1, q], state[:, q], start=True, stop=True).then_inc(yoff_in_psum[q], 1)

            def states(k, q):
                kn, qn = (k, 1) if q == 0 else (k + 1, 0)
                if live(kn):
                    pe.wait_ge(xsb_done[qn], kn + 1)
                else:
                    pe.wait_ge(state_done[0], k + 1)
                pe.wait_ge(xw_done[q], k + 1)
                pe.wait_ge(bg_read[q], k + 1)
                mul(xt_bank[:, :], btg[:, q, 0:P], xw[:, q], start=True, stop=True).then_inc(st_in_psum[q], 1)

            def y_diag(k, q):
                if begun(k - 1 + q):
                    pe.wait_ge(yts_done[1 - q], k + q)
                pe.wait_ge(xdt_done[q], k + 1)
                for h in range(H):
                    if h % 4 == 0:
                        pe.wait_ge(m_done[q][h // 4], k + 1)
                    last = mul(yd_bank[:, h * HD:(h + 1) * HD], mm[:, q, h], xdt[:, q, h * HD:(h + 1) * HD],
                               start=True, stop=True)
                last.then_inc(yd_in_psum[q], 1)

            def transpose_y(k, q):
                pe.wait_ge(yg_done[q], k + 1)
                for ki in range(KI):
                    last = tr(yd_bank[:, ki * P:(ki + 1) * P], yg[:, q, ki * P:(ki + 1) * P], ident[:, :])
                last.then_inc(yt_in_psum[q], 1)

            def out_project(k, q):
                pe.wait_ge(yts_done[q], k + 1)
                kn, qn = (k, 1) if q == 0 else (k + 1, 0)
                if live(kn):
                    pe.wait_ge(t1_done[qn], kn + 1)
                else:
                    pe.wait_ge(h_done[1 - q], k + 1)
                for ki in range(KI):
                    last = mul(yoff_bank[:, 0:D], yts[:, q, ki], wo[:, ki], start=ki == 0, stop=ki == KI - 1)
                last.then_inc(o_in_psum[q], 1)

            def one_pass(k, b):
                b2, bo = (b + 2) % BUF, (b - 1) % BUF
                if live(k + 1):
                    branch_project(k + 1, 1)
                if live(k):
                    sums(k)
                if live(k - 1):
                    transpose_y(k - 1, 0)
                    y_off(k - 1, bo, 1)
                if live(k + 1):
                    branch_project(k + 1, 0)
                    conv_project(k + 1, 1)
                    conv_project(k + 1, 0)
                if live(k - 1):
                    y_diag(k - 1, 1)
                if live(k):
                    b_and_g(k, b, 0)
                    exponents(k, 0, 0)
                if live(k - 1):
                    out_project(k - 1, 0)
                if live(k):
                    x_tokens(k, b, 0)
                    b_and_g(k, b, 1)
                    exponents(k, 0, 1)
                if live(k - 1):
                    transpose_y(k - 1, 1)
                if live(k):
                    y_off(k, b, 0)
                if live(k - 1):
                    states(k - 1, 1)
                if live(k + 1):
                    z_project(k + 1, 0)
                    conv_project(k + 1, 2)
                if live(k):
                    x_tokens(k, b, 1)
                if live(k - 1):
                    out_project(k - 1, 1)
                if live(k):
                    exponents(k, 1, 1)
                if live(k + 1):
                    z_project(k + 1, 1)
                if live(k):
                    exponents(k, 1, 0)
                if live(k + 2):
                    transpose_x(k + 2, b2)
                if live(k):
                    y_diag(k, 0)
                    states(k, 0)

            passes(pe, one_pass)


def kernel(**inputs):
    import numpy as _np
    import concourse.bacc as _bacc
    from concourse import mybir as _mybir
    from concourse.bass_utils import run_bass_kernel_spmd as _run

    a = {n: _np.asarray(v) for n, v in inputs.items()}
    laid_out = {
        "x": a["L0_attn_hidden_states"],
        "w_in": a["L0_attn_W_in"],
        "conv_w": a["L0_attn_conv_w"],
        "conv_b": a["L0_attn_conv_b"].reshape(-1, 128).T,
        "dt_bias": a["L0_attn_dt_bias"],
        "a_log": a["L0_attn_A_log"],
        "d_skip": a["L0_attn_D"],
        "rms_w": a["L0_attn_rms_w"].reshape(-1, 128).T,
        "w_out": a["L0_attn_W_out"],
        "ln_g": a["L0_attn_ln_g"],
        "ln_b": a["L0_attn_ln_b"],
        "f1t": a["L0_ffn_weight"].T,
        "f2t": a["L0_ffn_aux_weight1"].T,
        "f3": a["L0_ffn_aux_weight2"],
        "f_bias": a["L0_ffn_bias"],
    }
    nc = _bacc.Bacc("TRN2", target_bir_lowering=False, num_devices=1)
    arrays, args = {}, []
    for name, value in laid_out.items():
        value = _np.ascontiguousarray(value)
        arrays[f"in_{name}_dram"] = value
        args.append(nc.dram_tensor(f"in_{name}_dram", value.shape, _mybir.dt.from_np(value.dtype), kind="ExternalInput").ap())
    args.append(nc.dram_tensor("out_0_dram", laid_out["x"].shape, _mybir.dt.float32, kind="ExternalOutput").ap())
    program(nc, *args)
    r = _run(nc, [arrays], core_ids=[0])
    return r.results[0]["out_0_dram"]
```
